# Optimizing a Trainium2 kernel written in Bass

```python
import numpy as np
import jax
import jax.numpy as jnp

def _softmax(x, axis=-1):
    return jax.nn.softmax(x, axis=axis)

def _gelu(x):
    return jax.nn.gelu(x, approximate=True)

def _silu(x):
    return jax.nn.silu(x)

def _sigmoid(x):
    return jax.nn.sigmoid(x)

def _layernorm(x, axis=-1, eps=1e-05):
    m = jnp.mean(x, axis=axis, keepdims=True)
    v = jnp.var(x, axis=axis, keepdims=True)
    return (x - m) / jnp.sqrt(v + eps)

def _scatter_add(tgt, idx, src, axis=0):
    return tgt.at[idx].add(src)

def _segment_sum(src, seg, n):
    return jax.ops.segment_sum(src, seg, n)
kernel_name = 'mk_macaron_d1_jaxref_r8_4f74c4'

def setup_inputs(seed: int=0):
    np.random.seed(seed)
    _w = jnp.asarray

    def _L0_attn_setup():
        import jax, jax.numpy as jnp
        import numpy as np
        DIM = 128
        HEADS = 16
        DIM_HEAD = 64
        WINDOW = 32
        NEG = -1000000000.0

        def rms_norm(x, gamma, size):
            nrm = jnp.sqrt(jnp.sum(x * x, axis=-1, keepdims=True))
            return x / jnp.maximum(nrm, 1e-12) * size ** 0.5 * gamma

        def sliding_window_attention(q, k, v, window):
            b, h, S, d = q.shape
            Bk = window
            nb = S // Bk
            qb = q.reshape(b, h, nb, Bk, d)
            kb = k.reshape(b, h, nb, Bk, d)
            vb = v.reshape(b, h, nb, Bk, d)
            k_prev = jnp.pad(kb, ((0, 0), (0, 0), (1, 0), (0, 0), (0, 0)))[:, :, :nb]
            v_prev = jnp.pad(vb, ((0, 0), (0, 0), (1, 0), (0, 0), (0, 0)))[:, :, :nb]
            kctx = jnp.concatenate([k_prev, kb], axis=3)
            vctx = jnp.concatenate([v_prev, vb], axis=3)
            scale = 1.0 / jnp.sqrt(jnp.asarray(d, q.dtype))
            scores = jnp.einsum('bhnqd,bhnkd->bhnqk', qb, kctx) * scale
            qi = jnp.arange(Bk)[:, None]
            kj = jnp.arange(2 * Bk)[None, :]
            diff = Bk + qi - kj
            base = (diff >= 0) & (diff <= window)
            blk = jnp.arange(nb)[:, None, None]
            key_exists = (blk - 1) * Bk + kj[None] >= 0
            mask = base[None] & key_exists
            scores = jnp.where(mask[None, None], scores, NEG)
            attn = jax.nn.softmax(scores, axis=-1)
            out = jnp.einsum('bhnqk,bhnkd->bhnqd', attn, vctx)
            return out.reshape(b, h, S, d)
        key = jax.random.key(seed)
        ks = jax.random.split(key, 6)
        b, S = (2, 512)
        dim_inner = HEADS * DIM_HEAD
        x = jax.random.normal(ks[0], (b, S, DIM), dtype=jnp.float32)
        gamma = jnp.ones((DIM,), dtype=jnp.float32)
        W_qkv = jax.random.normal(ks[1], (DIM, 3 * dim_inner), dtype=jnp.float32) * 0.02
        W_gates = jax.random.normal(ks[2], (DIM, HEADS), dtype=jnp.float32) * 0.02
        b_gates = jnp.zeros((HEADS,), dtype=jnp.float32)
        W_out = jax.random.normal(ks[3], (dim_inner, DIM), dtype=jnp.float32) * 0.02
        return {'x': x, 'gamma': gamma, 'W_qkv': W_qkv, 'W_gates': W_gates, 'b_gates': b_gates, 'W_out': W_out}
    _L0_attn_in = _L0_attn_setup()

    def _L0_ffn_setup():
        import jax, jax.numpy as jnp
        import numpy as np
        DIM = 128

        def _reference_tuple_inner(x, W_r, W_k, W_v, mu_r, mu_k):
            B, T, C = x.shape
            x_prev = jnp.concatenate([jnp.zeros((B, 1, C), x.dtype), x[:, :-1, :]], axis=1)
            xr = mu_r * x + (1.0 - mu_r) * x_prev
            xk = mu_k * x + (1.0 - mu_k) * x_prev
            r = jax.nn.sigmoid(jnp.einsum('btc,dc->btd', xr, W_r))
            k = jnp.einsum('btc,dc->btd', xk, W_k)
            k_act = jnp.square(jax.nn.relu(k))
            out = r * jnp.einsum('btc,dc->btd', k_act, W_v)
            new_state = x[:, -1, :]
            return (out, new_state)
        key = jax.random.key(seed)
        ks = jax.random.split(key, 6)
        B, T, C = (8, 256, DIM)
        x = jax.random.normal(ks[0], (B, T, C), dtype=jnp.float32)
        s = 1.0 / np.sqrt(C)
        W_r = jax.random.uniform(ks[1], (C, C), jnp.float32, -s, s)
        W_k = jax.random.uniform(ks[2], (C, C), jnp.float32, -s, s)
        W_v = jax.random.uniform(ks[3], (C, C), jnp.float32, -s, s)
        mu_r = jax.random.uniform(ks[4], (C,), jnp.float32)
        mu_k = jax.random.uniform(ks[5], (C,), jnp.float32)
        return {'x': x, 'W_r': W_r, 'W_k': W_k, 'W_v': W_v, 'mu_r': mu_r, 'mu_k': mu_k}
    _L0_ffn_in = _L0_ffn_setup()
    _d = {'L0_attn_x': _L0_attn_in['x'], 'L0_attn_gamma': _L0_attn_in['gamma'], 'L0_attn_W_qkv': _L0_attn_in['W_qkv'], 'L0_attn_W_gates': _L0_attn_in['W_gates'], 'L0_attn_b_gates': _L0_attn_in['b_gates'], 'L0_attn_W_out': _L0_attn_in['W_out'], 'L0_ffn_W_r': _L0_ffn_in['W_r'], 'L0_ffn_W_k': _L0_ffn_in['W_k'], 'L0_ffn_W_v': _L0_ffn_in['W_v'], 'L0_ffn_mu_r': _L0_ffn_in['mu_r'], 'L0_ffn_mu_k': _L0_ffn_in['mu_k']}
    _x0 = _d['L0_attn_x']
    _d['L0_attn_x'] = jax.random.normal(jax.random.fold_in(jax.random.key(seed), 1), (32, 256, 128), dtype=_x0.dtype)
    del _x0
    return _d

def reference(L0_attn_x, L0_attn_gamma, L0_attn_W_qkv, L0_attn_W_gates, L0_attn_b_gates, L0_attn_W_out, L0_ffn_W_r, L0_ffn_W_k, L0_ffn_W_v, L0_ffn_mu_r, L0_ffn_mu_k):

    def _L0_attn_ref(x, gamma, W_qkv, W_gates, b_gates, W_out):
        import jax, jax.numpy as jnp
        import numpy as np
        DIM = 128
        HEADS = 16
        DIM_HEAD = 64
        WINDOW = 32
        NEG = -1000000000.0

        def rms_norm(x, gamma, size):
            nrm = jnp.sqrt(jnp.sum(x * x, axis=-1, keepdims=True))
            return x / jnp.maximum(nrm, 1e-12) * size ** 0.5 * gamma

        def sliding_window_attention(q, k, v, window):
            b, h, S, d = q.shape
            Bk = window
            nb = S // Bk
            qb = q.reshape(b, h, nb, Bk, d)
            kb = k.reshape(b, h, nb, Bk, d)
            vb = v.reshape(b, h, nb, Bk, d)
            k_prev = jnp.pad(kb, ((0, 0), (0, 0), (1, 0), (0, 0), (0, 0)))[:, :, :nb]
            v_prev = jnp.pad(vb, ((0, 0), (0, 0), (1, 0), (0, 0), (0, 0)))[:, :, :nb]
            kctx = jnp.concatenate([k_prev, kb], axis=3)
            vctx = jnp.concatenate([v_prev, vb], axis=3)
            scale = 1.0 / jnp.sqrt(jnp.asarray(d, q.dtype))
            scores = jnp.einsum('bhnqd,bhnkd->bhnqk', qb, kctx) * scale
            qi = jnp.arange(Bk)[:, None]
            kj = jnp.arange(2 * Bk)[None, :]
            diff = Bk + qi - kj
            base = (diff >= 0) & (diff <= window)
            blk = jnp.arange(nb)[:, None, None]
            key_exists = (blk - 1) * Bk + kj[None] >= 0
            mask = base[None] & key_exists
            scores = jnp.where(mask[None, None], scores, NEG)
            attn = jax.nn.softmax(scores, axis=-1)
            out = jnp.einsum('bhnqk,bhnkd->bhnqd', attn, vctx)
            return out.reshape(b, h, S, d)
        b, S, dim = x.shape
        xn = rms_norm(x, gamma, dim)
        qkv = xn @ W_qkv
        qkv = qkv.reshape(b, S, 3, HEADS, DIM_HEAD)
        q, k, v = [jnp.transpose(t, (0, 2, 1, 3)) for t in (qkv[:, :, 0], qkv[:, :, 1], qkv[:, :, 2])]
        out = sliding_window_attention(q, k, v, WINDOW)
        gates = xn @ W_gates + b_gates
        out = out * jax.nn.sigmoid(jnp.transpose(gates, (0, 2, 1)))[..., None]
        out = jnp.transpose(out, (0, 2, 1, 3)).reshape(b, S, HEADS * DIM_HEAD)
        return out @ W_out

    def _L0_ffn_ref(x, W_r, W_k, W_v, mu_r, mu_k):
        import jax, jax.numpy as jnp
        import numpy as np
        DIM = 128

        def _reference_tuple_inner(x, W_r, W_k, W_v, mu_r, mu_k):
            B, T, C = x.shape
            x_prev = jnp.concatenate([jnp.zeros((B, 1, C), x.dtype), x[:, :-1, :]], axis=1)
            xr = mu_r * x + (1.0 - mu_r) * x_prev
            xk = mu_k * x + (1.0 - mu_k) * x_prev
            r = jax.nn.sigmoid(jnp.einsum('btc,dc->btd', xr, W_r))
            k = jnp.einsum('btc,dc->btd', xk, W_k)
            k_act = jnp.square(jax.nn.relu(k))
            out = r * jnp.einsum('btc,dc->btd', k_act, W_v)
            new_state = x[:, -1, :]
            return (out, new_state)
        return _reference_tuple_inner(x, W_r, W_k, W_v, mu_r, mu_k)[0]
    x = L0_attn_x
    x = x + 0.5 * _L0_ffn_ref(_layernorm(x, axis=-1), L0_ffn_W_r, L0_ffn_W_k, L0_ffn_W_v, L0_ffn_mu_r, L0_ffn_mu_k)
    x = x + _L0_attn_ref(_layernorm(x, axis=-1), L0_attn_gamma, L0_attn_W_qkv, L0_attn_W_gates, L0_attn_b_gates, L0_attn_W_out)
    x = x + 0.5 * _L0_ffn_ref(_layernorm(x, axis=-1), L0_ffn_W_r, L0_ffn_W_k, L0_ffn_W_v, L0_ffn_mu_r, L0_ffn_mu_k)
    return x

_drawn_inputs = setup_inputs


def setup_inputs(seed=0):
    import zlib

    import numpy as np

    out = dict(_drawn_inputs(seed))
    spreads = {'L0_attn_gamma': (1.0, 0.6), 'L0_attn_b_gates': (0.0, 0.8)}
    factors = {'L0_attn_W_qkv': 3.493,
     'L0_attn_W_gates': 8.0,
     'L0_attn_W_out': 3.502,
     'L0_ffn_W_r': 3.166,
     'L0_ffn_mu_r': 6.216}
    for name, (base, spread) in spreads.items():
        noise = np.random.default_rng([zlib.crc32(name.encode()), seed]).standard_normal(out[name].shape)
        drawn = base * np.exp(spread * noise) if base else spread * noise
        out[name] = jnp.asarray(drawn.astype(out[name].dtype))
    for name, factor in factors.items():
        out[name] = (out[name] * factor).astype(out[name].dtype)
    return out
```

```python
import numpy as np
import concourse.bass as bass
from concourse import mybir
from contextlib import ExitStack

TOKENS, DIM, HEADS, HEAD_DIM = 8192, 128, 16, 64
SEQ, WINDOW = 256, 32
GROUP = 512
GROUPS = TOKENS // GROUP
TILES = GROUP // 128
BLOCKS = GROUP // WINDOW
QUADS = BLOCKS // 4
HQ = HEADS * WINDOW
EPS = 1e-5
NEG = -1e30
T_HEADS = [range(0, 6), range(6, 11), range(11, 16), range(0)]
C_IDENT, C_EYE, C_MASK, C_BLOCK, C_LOW, C_END = 0, 128, 160, 224, 352, 353


def constants():
    p = np.arange(128)
    c = np.zeros((128, C_END), np.float32)
    c[:, C_IDENT:C_IDENT + 128] = np.eye(128)
    c[:, C_EYE:C_EYE + 32] = (p[:, None] % 32) == np.arange(32)[None]
    key, query = p[:, None] % 64, np.arange(32)[None]
    seen = (key >= query) & (key <= query + WINDOW)
    c[:, C_MASK:C_MASK + 32] = np.where(seen, 0.0, NEG)
    c[:, C_MASK + 32:C_MASK + 64] = np.where(seen & ((p[:, None] >= 64) | (key >= 32)), 0.0, NEG)
    c[:, C_BLOCK:C_BLOCK + 128] = (p[:, None] // 64) == (p[None] // 64)
    c[:, C_LOW] = (p // 32) % 2
    return c


def macaron(nc, x_in, gamma, w_qkv, w_gates, b_gates, w_out, w_r, w_k, w_v, mu_r, mu_k, consts, out):
    dt = mybir.dt
    f32, f32r, bf16, f16, i32 = dt.float32, dt.float32r, dt.bfloat16, dt.float16, dt.int32
    ALU, ACT, AX = mybir.AluOpType, mybir.ActivationFunctionType, mybir.AxisListType

    x_tiles = x_in.rearrange("b (n p) c -> p (b n) c", p=128)
    out_tiles = out.rearrange("b (n p) c -> p (b n) c", p=128)

    ctx = ExitStack()
    with ctx:
        def sb(name, shape, dtype=f32):
            return ctx.enter_context(nc.sbuf_tensor(name, shape, dtype))

        def sem(name):
            return ctx.enter_context(nc.semaphore(name))

        cst = sb("cst", [128, C_END])
        ident = cst[:, C_IDENT:C_IDENT + 128]
        eye = cst[:, C_EYE:C_EYE + 32]
        ident_bf = sb("ident_bf", [128, 128], bf16)
        mask_bf = sb("mask_bf", [128, 2, 32], bf16)
        minus_bf = sb("minus_bf", [128, 128], bf16)
        ones_r = sb("ones_r", [128, 128], f32r)
        minus_low = sb("minus_low", [128, 1])
        gam = sb("gam", [128, 1])
        mu = sb("mu", [128, 2])
        gate_bias = sb("gate_bias", [128, HEADS])
        wg = sb("wg", [128, HEADS])
        fold_qk = sb("fold_qk", [128, HEADS, 128])
        fold_vo = sb("fold_vo", [128, HEADS, 128])
        ffn_wT = sb("ffn_wT", [128, 3, 128])
        x = sb("x", [128, TOKENS // 128, DIM])
        t = [sb(f"t{i}", [128, HEADS, GROUP]) for i in range(2)]
        zT = [sb(f"zT{i}", [128, WINDOW + GROUP]) for i in range(2)]
        zk_hi = [sb(f"zk_hi{i}", [128, BLOCKS, DIM], f16) for i in range(2)]
        zk_lo = [sb(f"zk_lo{i}", [128, BLOCKS, DIM], f16) for i in range(2)]
        keys_twice = sb("keys_twice", [128, BLOCKS, 2, 64])
        queries_twice = sb("queries_twice", [128, BLOCKS, 2, 32])
        U = sb("U", [128, HEADS, 4, WINDOW])
        P = sb("P", [128, 2 * HQ])
        P_even = sb("P_even", [128, 2, HQ], f16)
        P_odd = sb("P_odd", [128, 2, HQ], f16)
        shift_rows = sb("shift_rows", [128, 2, HQ], bf16)
        factor_rows = sb("factor_rows", [128, 2, HQ], f32r)
        half = sb("half", [128, 32])
        swapped = sb("swapped", [128, 32])
        m_full = sb("m_full", [128, 32])
        m_hi = sb("m_hi", [128, 32], bf16)
        m_parts = sb("m_parts", [128, 32], bf16)
        den = sb("den", [128, 32])
        f_full = sb("f_full", [128, 32])
        f_hi = sb("f_hi", [128, 32], f32r)
        f_parts = sb("f_parts", [128, 32])
        gate = [sb(f"gate{i}", [128, 8, HEADS]) for i in range(2)]
        stats = sb("stats", [128, TILES, 6])
        mean_var = sb("mean_var", [128, TILES, 2])
        ra, ry, rt, rscale, rbias = (sb(n, [128, TILES]) for n in ("ra", "ry", "rt", "rscale", "rbias"))
        pause = sb("pause", [128, 1])
        y = [sb(f"y{i}", [128, TILES, DIM]) for i in range(2)]
        yT = [sb(f"yT{i}", [128, 2, SEQ + 1]) for i in range(2)]
        xr = [sb(f"xr{i}", [128, GROUP]) for i in range(2)]
        xk = [sb(f"xk{i}", [128, GROUP]) for i in range(2)]
        kact = [sb(f"kact{i}", [128, GROUP]) for i in range(2)]
        tanh_r = [sb(f"tanh_r{i}", [128, GROUP]) for i in range(2)]
        z = y[0]
        stage = t[1][:, :, :].rearrange("p h n -> p (h n)")
        wqkv_st = stage[:, 0:3072]
        wT_st = stage[:, 3072:6144].rearrange("p (j c) -> p j c", c=128)
        wout_st = stage[:, 6144:7168].rearrange("p (j c) -> p j c", c=128)
        ffn_st = stage[:, 7168:7552].rearrange("p (j c) -> p j c", c=128)

        ps = ctx.enter_context(nc.psum_tensor("ps", [128, 8, 512], f32))
        S = [ps[:, 0:2, :], ps[:, 2:4, :]]
        prod = [ps[:, 4, :], ps[:, 5, :]]
        obank = ps[:, 6, 0:128]
        wbank = ps[:, 7, :]

        s_const, s_weights, s_load0, s_load1, s_loadrest = (sem(n) for n in ("s_const", "s_weights", "s_load0", "s_load1", "s_loadrest"))
        s_prep, s_scaled, s_tr, s_trc, s_fold, s_set = (sem(n) for n in ("s_prep", "s_scaled", "s_tr", "s_trc", "s_fold", "s_set"))
        s_pad = sem("s_pad")
        s_scores, s_m, s_shiftrows, s_shift, s_exp = (sem(n) for n in ("s_scores", "s_m", "s_shiftrows", "s_shift", "s_exp"))
        s_f, s_factorrows, s_factor, s_p2 = (sem(n) for n in ("s_f", "s_factorrows", "s_factor", "s_p2"))
        s_prod, s_evac, s_out, s_outadd = (sem(n) for n in ("s_prod", "s_evac", "s_out", "s_outadd"))
        s_z, s_zTp, s_zT, s_zkp, s_zkhi, s_zklo = (sem(n) for n in ("s_z", "s_zTp", "s_zT", "s_zkp", "s_zkhi", "s_zklo"))
        s_gp, s_g, s_gexp = (sem(n) for n in ("s_gp", "s_g", "s_gexp"))
        s_y, s_yTp, s_yT, s_mix, s_kp, s_relu, s_kact, s_rp, s_th, s_vp, s_gv, s_x = (
            [sem(f"{n}{i + 1}") for i in range(2)]
            for n in ("s_y", "s_yTp", "s_yT", "s_mix", "s_kp", "s_relu", "s_kact", "s_rp", "s_th", "s_vp", "s_gv", "s_x"))
        s_twice = sem("s_twice")
        s_link, s_store = sem("s_link"), sem("s_store")

        def attends(s):
            return 0 <= s < GROUPS

        def exists(s, q):
            return 0 <= QUADS * s + q + 1 < QUADS * GROUPS

        def products_before(g):
            return HEADS + (HEADS + BLOCKS) * g

        def loop_slots(engine, slot):
            for s in (-2, -1, 0, 1):
                slot(s, s)
            with engine.Fori(0, 6) as it:
                for k in range(2):
                    slot(it * 2 + (2 + k), 2 + k)
            for s in (14, 15, 16):
                slot(s, s)

        block = ctx.enter_context(nc.Block())

        @block.sync
        def _(sp):
            sp.dma_start(cst[:, :], consts).then_inc(s_const, 16)
            sp.dma_start(wqkv_st, w_qkv).then_inc(s_weights, 16)
            sp.dma_start(wout_st, w_out.rearrange("(j p) c -> p j c", p=128)).then_inc(s_weights, 16)
            sp.dma_start(x[:, 0:TILES, :], x_tiles[:, 0:TILES, :]).then_inc(s_load0, 16)
            sp.dma_start(x[:, TILES:2 * TILES, :], x_tiles[:, TILES:2 * TILES, :]).then_inc(s_load1, 16)
            sp.dma_start(x[:, 2 * TILES:, :], x_tiles[:, 2 * TILES:, :]).then_inc(s_loadrest, 16)
            with sp.Fori(0, GROUPS) as g:
                sp.wait_ge(s_x[1], g + 1)
                sp.dma_start(out_tiles[:, bass.ts(g, TILES), :], x[:, bass.ts(g, TILES), :]).then_inc(s_store, 16)
            sp.wait_ge(s_store, 16 * GROUPS)

        @block.tensor
        def _(pe):
            mm = pe.matmul
            pe.wait_ge(s_const, 16)
            pe.wait_ge(s_prep, 1)
            for j in range(3):
                i = pe.transpose(wbank[:, 128 * j:128 * j + 128], ffn_st[:, j, :], ident)
            i.then_inc(s_tr, 1)
            pe.wait_ge(s_scaled, 1)
            for b in range(6):
                for j in range(4):
                    c = 128 * (4 * b + j)
                    i = pe.transpose(ps[:, b, 128 * j:128 * j + 128], wqkv_st[:, c:c + 128], ident)
                i.then_inc(s_tr, 1)
            pe.wait_ge(s_trc, 7)
            for k, (a, b) in enumerate(((lambda j: wT_st[:, j, :], lambda j: wT_st[:, 8 + j, :]),
                                        (lambda j: wT_st[:, 16 + j, :], lambda j: wout_st[:, j, :]))):
                for h in range(HEADS):
                    j, r = h // 2, (h % 2) * 64
                    bank, col = 4 * k + 2 * (h % 2) + j // 4, 128 * (j % 4)
                    i = mm(ps[:, bank, col:col + 128], a(j)[r:r + 64, :], b(j)[r:r + 64, :], start=True, stop=True)
                i.then_inc(s_fold, 1)
            pe.wait_ge(s_set, 2)

            release = [None]

            def take_work_bank():
                if release[0] is not None:
                    pe.wait_ge(*release[0])

            def work_transposes(src, done, value, freed, made, made_value):
                pe.wait_ge(made, made_value)
                take_work_bank()
                for i in range(TILES):
                    op = pe.transpose(wbank[:, 128 * i:128 * i + 128], src[:, i, :], ident)
                op.then_inc(done, 1)
                release[0] = (freed, value)

            def slot(g, s):
                has_next, has_ffn1, has_ffn2 = attends(s + 1), attends(s + 2), attends(s - 1)
                cur, nxt = s % 2, (s + 1) % 2
                if s > -2:
                    release[0] = (s_zT, g + 2) if has_next else (s_gv[1], g - 1)
                count = [0]

                def product(n_done):
                    if s >= 0:
                        n = products_before(g) + count[0]
                    else:
                        n = count[0]
                    if s >= 0 or count[0] >= 2:
                        pe.wait_ge(s_evac, n - 1)
                    bank = prod[count[0] % 2]
                    count[0] += 1
                    return bank

                def zk(j):
                    if not has_next:
                        return
                    if j == 0:
                        pe.wait_ge(s_twice, g + 2)
                    take_work_bank()
                    for i in range(4):
                        b = 4 * j + i
                        keys = keys_twice[:, b, :, :].rearrange("p a k -> p (a k)")
                        op = pe.transpose(wbank[:, 128 * i:128 * i + 128], keys, ident)
                    op.then_inc(s_zkp, 1)
                    release[0] = (s_zklo, 4 * (g + 1) + j + 1)

                def gates():
                    if not has_next:
                        return
                    take_work_bank()
                    for i in range(8):
                        qs = queries_twice[:, 2 * i:2 * i + 2, :, :].rearrange("p b a q -> p (b a q)")
                        op = mm(wbank[:, 16 * i:16 * i + 16], qs, wg[:, :], start=True, stop=True)
                    op.then_inc(s_gp, 1)
                    release[0] = (s_g, g + 2)

                def ffn(layer, gg, stage_):
                    if not (has_ffn1 if layer == 0 else has_ffn2):
                        return
                    if stage_ == "T":
                        return work_transposes(y[layer], s_yTp[layer], gg + 1, s_yT[layer], s_y[layer], gg + 1)
                    if stage_ == "k":
                        pe.wait_ge(s_mix[layer], gg + 1)
                        take_work_bank()
                        mm(wbank, ffn_wT[:, 1, :], xk[layer][:, :], start=True, stop=True).then_inc(s_kp[layer], 1)
                        release[0] = (s_relu[layer], gg + 1)
                    if stage_ == "r":
                        take_work_bank()
                        for i in range(TILES):
                            c = slice(128 * i, 128 * i + 128)
                            op = mm(wbank[:, c], xr[layer][:, c], ffn_wT[:, 0, :], start=True, stop=True)
                        op.then_inc(s_rp[layer], 1)
                        release[0] = (s_th[layer], gg + 1)
                    if stage_ == "v":
                        pe.wait_ge(s_kact[layer], gg + 1)
                        take_work_bank()
                        for i in range(TILES):
                            c = slice(128 * i, 128 * i + 128)
                            op = mm(wbank[:, c], kact[layer][:, c], ffn_wT[:, 2, :], start=True, stop=True)
                        op.then_inc(s_vp[layer], 1)
                        release[0] = (s_gv[layer], gg + 1)

                def z_transposes():
                    if has_ffn1:
                        work_transposes(z, s_zTp, g + 3, s_zT, s_z, g + 3)

                none = lambda: None
                work = [[lambda: zk(0), lambda: zk(1), lambda: zk(2), lambda: zk(3)],
                        [lambda: ffn(0, g + 2, "T"), lambda: ffn(1, g - 1, "T"), gates, lambda: ffn(0, g + 2, "k")],
                        [lambda: ffn(0, g + 2, "r"), lambda: ffn(0, g + 2, "v"), lambda: ffn(1, g - 1, "k"),
                         lambda: ffn(1, g - 1, "r")],
                        [lambda: ffn(1, g - 1, "v"), none, z_transposes, none]]

                for q in range(QUADS):
                    quad = QUADS * g + q
                    new = exists(s, q)
                    nq, par = (q + 1) % 4, (q + 1) % 2
                    own = cur if q < 3 else nxt
                    if new:
                        for i in range(2):
                            first = nq % 2 == 0 and i == 0
                            band = mask_bf[:, int(first), :].unsqueeze(1).to_broadcast([128, HEADS, 32])
                            mm(S[par][:, i, :], ident_bf[:, :], band, start=True, stop=False, skip_group_check=True)
                        if q == 3:
                            if s >= 0:
                                pe.wait_ge(s_evac, products_before(g) + count[0])
                            else:
                                pe.wait_ge(s_evac, HEADS)
                        for i in range(2):
                            for j in range(2):
                                b = 4 * nq + 2 * i + j
                                op = mm(S[par][64 * j:64 * j + 64, i, :], zT[own][:, 32 * b:32 * b + 64],
                                        t[own][:, :, 32 * b:32 * b + 32], start=False, stop=True, skip_group_check=True)
                        op.then_inc(s_scores, 1)
                    work[q][0]()
                    if attends(s):
                        if q == 0:
                            pe.wait_ge(s_zklo, 4 * g + 4)
                        pe.wait_ge(s_p2, quad + 1)
                        for b in range(4):
                            bank = product(1)
                            probs = (P_odd if b % 2 else P_even)[:, b // 2, :]
                            mm(bank, zk_hi[cur][:, 4 * q + b, :], probs, start=True, stop=False)
                            mm(bank, zk_lo[cur][:, 4 * q + b, :], probs, start=False, stop=True).then_inc(s_prod, 1)
                    if new:
                        pe.wait_ge(s_shiftrows, quad + 2)
                        for i in range(2):
                            op = mm(S[par][:, i, :], minus_bf[:, :], shift_rows[:, i, :], start=False, stop=True,
                                    skip_group_check=True)
                        op.then_inc(s_shift, 1)
                    work[q][1]()
                    if has_next:
                        for h in T_HEADS[q]:
                            bank = product(1)
                            mm(bank, fold_qk[:, h, :], zT[nxt][:, WINDOW:], start=True, stop=True).then_inc(s_prod, 1)
                    work[q][2]()
                    if new:
                        pe.wait_ge(s_factorrows, quad + 2)
                        for i in range(2):
                            op = mm(S[par][:, i, :], ones_r[:, :], factor_rows[:, i, :], start=True, stop=True)
                        op.then_inc(s_factor, 1)
                    work[q][3]()
                    if attends(s):
                        u_last = sum(4 + len(T_HEADS[k]) * has_next for k in range(q)) + 4
                        pe.wait_ge(s_evac, products_before(g) + u_last)
                        if s > 0 or q > 0:
                            pe.wait_ge(s_outadd, quad)
                        for h in range(HEADS):
                            op = mm(obank, U[:, h, :, :].rearrange("p b q -> p (b q)"), fold_vo[:, h, :],
                                    start=(h == 0), stop=(h == HEADS - 1))
                        op.then_inc(s_out, 1)

            loop_slots(pe, slot)

        @block.scalar
        def _(act):
            def wait(sem_, value):
                act.wait_ge(sem_, value)
                act.wait_ge(s_const, 16)

            act.dma_start(ffn_st[:, 0, :], w_r).then_inc(s_weights, 16)
            act.dma_start(ffn_st[:, 1, :], w_k).then_inc(s_weights, 16)
            act.dma_start(ffn_st[:, 2, :], w_v).then_inc(s_weights, 16)
            act.dma_start(gam[:, :], gamma.rearrange("(p a) -> p a", a=1)).then_inc(s_weights, 16)
            act.dma_start(mu[:, 0:1], mu_r.rearrange("(p a) -> p a", a=1)).then_inc(s_weights, 16)
            act.dma_start(mu[:, 1:2], mu_k.rearrange("(p a) -> p a", a=1)).then_inc(s_weights, 16)
            act.dma_start(wg[:, :], w_gates).then_inc(s_weights, 16)
            act.dma_start(gate_bias[:, :], b_gates.rearrange("(a h) -> a h", a=1).partition_broadcast(128)
                          if False else b_gates.rearrange("(a h) -> a h", a=1).to_broadcast([128, HEADS])).then_inc(s_weights, 16)
            act.wait_ge(s_tr, 1)
            act.activation(ffn_wT[:, 0:2, :], wbank[:, 0:256].rearrange("p (j c) -> p j c", c=128), ACT.Copy)
            act.activation(ffn_wT[:, 2, :], wbank[:, 256:384], ACT.Copy, scale=0.25).then_inc(s_trc, 1)
            for b in range(6):
                act.wait_ge(s_tr, b + 2)
                act.activation(wT_st[:, 4 * b:4 * b + 4, :], ps[:, b, :].rearrange("p (j c) -> p j c", c=128),
                               ACT.Copy).then_inc(s_trc, 1)
            for k, (dst, scale) in enumerate(((fold_qk, HEAD_DIM ** -0.5), (fold_vo, 1.0))):
                act.wait_ge(s_fold, k + 1)
                for odd in range(2):
                    for hb in range(2):
                        heads = dst[:, 8 * hb + odd:8 * hb + odd + 7:2, :]
                        op = act.activation(heads, ps[:, 4 * k + 2 * odd + hb, :].rearrange("p (j c) -> p j c", c=128),
                                            ACT.Copy, scale=scale)
                op.then_inc(s_set, 1)
            act.wait_ge(s_pad, 1)

            def slot(g, s):
                has_next, has_ffn1, has_ffn2 = attends(s + 1), attends(s + 2), attends(s - 1)
                cur, nxt = s % 2, (s + 1) % 2
                count = [0]

                def evacuate(dst, by_head=False):
                    n = (products_before(g) if s >= 0 else 0) + count[0]
                    wait(s_prod, n + 1)
                    src = prod[count[0] % 2]
                    if by_head:
                        src = src.rearrange("p (h q) -> p h q", q=WINDOW)
                    act.activation(dst, src, ACT.Copy).then_inc(s_evac, 1)
                    count[0] += 1

                def zk(j):
                    if has_next:
                        wait(s_zkp, 4 * (g + 1) + j + 1)
                        act.activation(zk_hi[nxt][:, 4 * j:4 * j + 4, :], wbank.rearrange("p (b c) -> p b c", c=128),
                                       ACT.Copy).then_inc(s_zkhi, 1)

                def ffn(layer, gg, stage_):
                    if not (has_ffn1 if layer == 0 else has_ffn2):
                        return
                    if stage_ == "T":
                        wait(s_yTp[layer], gg + 1)
                        act.activation(yT[layer][:, :, 1:], wbank.rearrange("p (b n) -> p b n", b=2),
                                       ACT.Copy).then_inc(s_yT[layer], 1)
                    if stage_ == "k":
                        wait(s_kp[layer], gg + 1)
                        act.activation(kact[layer][:, :], wbank, ACT.Relu).then_inc(s_relu[layer], 1)
                    if stage_ == "r":
                        if s + (2 if layer == 0 else -1) > 0:
                            wait(s_x[layer], gg)
                        wait(s_rp[layer], gg + 1)
                        act.activation(tanh_r[layer][:, :], wbank, ACT.Tanh, scale=0.5).then_inc(s_th[layer], 1)

                def z_out():
                    if has_ffn1:
                        wait(s_zTp, g + 3)
                        act.activation(zT[cur][:, WINDOW:], wbank, ACT.Copy).then_inc(s_zT, 1)

                def gates():
                    if has_next:
                        wait(s_g, g + 2)
                        act.activation(gate[nxt][:, :, :], gate[nxt][:, :, :], ACT.Exp, scale=-1.0).then_inc(s_gexp, 1)

                none = lambda: None
                work = [[lambda: zk(0), lambda: zk(1), lambda: zk(2), lambda: zk(3)],
                        [lambda: ffn(0, g + 2, "T"), lambda: ffn(1, g - 1, "T"), gates, lambda: ffn(0, g + 2, "k")],
                        [lambda: ffn(0, g + 2, "r"), none, lambda: ffn(1, g - 1, "k"), lambda: ffn(1, g - 1, "r")],
                        [none, none, z_out, none]]
                for q in range(QUADS):
                    quad = QUADS * g + q
                    work[q][0]()
                    if attends(s):
                        for b in range(4):
                            evacuate(U[:, :, b, :], True)
                    if exists(s, q):
                        if s >= 0:
                            wait(s_p2, quad + 1)
                        wait(s_shift, quad + 2)
                        act.activation(P[:, :], S[(q + 1) % 2].rearrange("p a n -> p (a n)"), ACT.Exp).then_inc(s_exp, 1)
                    work[q][1]()
                    if has_next:
                        if q == 0 and s > 0:
                            wait(s_scores, 4 * g)
                        for h in T_HEADS[q]:
                            evacuate(t[nxt][:, h, :])
                    work[q][2]()
                    work[q][3]()

            loop_slots(act, slot)

        @block.vector
        def _(dve):
            links = [0, 0]

            def link(op):
                links[0] += 1
                op.then_inc(s_link, 1)
                dve.wait_ge(s_link, links[0] + links[1])

            dve.memset(zT[0][:, 0:WINDOW], 0.0)
            dve.memset(zT[1][:, 0:WINDOW], 0.0)
            for i in range(2):
                op = dve.memset(yT[i][:, :, 0:1], 0.0)
            op.then_inc(s_pad, 1)
            dve.wait_ge(s_const, 16)
            dve.tensor_copy(ident_bf[:, :], ident)
            dve.tensor_copy(mask_bf[:, :, :], cst[:, C_MASK:C_MASK + 64].rearrange("p (k q) -> p k q", k=2))
            dve.tensor_scalar(minus_bf[:, :], cst[:, C_BLOCK:C_BLOCK + 128], -1.0, None, ALU.mult)
            dve.tensor_copy(ones_r[:, :], cst[:, C_BLOCK:C_BLOCK + 128])
            dve.tensor_scalar(minus_low[:, :], cst[:, C_LOW:C_LOW + 1], -1.0, None, ALU.mult)
            dve.wait_ge(s_weights, 16 * 10)
            link(dve.tensor_scalar(wg[:, :], wg[:, :], gam[:, 0:1], None, ALU.mult))
            dve.tensor_copy(rt[:, 0:1], gam[:, :]).then_inc(s_prep, 1)
            dve.tensor_scalar(wqkv_st, wqkv_st, gam[:, 0:1], None, ALU.mult).then_inc(s_scaled, 1)

            def reciprocal_root():
                link(dve.tensor_scalar(ry[:, :].bitcast(i32), ra[:, :].bitcast(i32), -0.5, float(0x5F3759DF),
                                       ALU.mult, ALU.add))
                for _ in range(4):
                    link(dve.tensor_tensor(rt[:, :], ry[:, :], ry[:, :], ALU.mult))
                    link(dve.scalar_tensor_tensor(rt[:, :], rt[:, :], -0.5, ra[:, :], ALU.mult, ALU.mult))
                    link(dve.scalar_tensor_tensor(ry[:, :], rt[:, :], 1.5, ry[:, :], ALU.add, ALU.mult))

            def statistics(first_tile):
                dve.memset(pause[:, :], 0.0)
                for i in range(TILES):
                    op = dve.bn_stats(stats[:, i, :], x[:, bass.ds(first_tile + i, 1), :])
                link(op)
                dve.memset(pause[:, :], 0.0)
                for i in range(TILES):
                    op = dve.bn_aggr(mean_var[:, i, :], stats[:, i, :])
                link(op)
                link(dve.tensor_scalar(ra[:, :], mean_var[:, :, 1], EPS, None, ALU.add))
                reciprocal_root()

            def normalise(dst, scale, first_tile, done):
                link(dve.scalar_tensor_tensor(rbias[:, :], mean_var[:, :, 0], -1.0, scale[:, :], ALU.mult, ALU.mult))
                for i in range(TILES):
                    op = dve.tensor_scalar(dst[:, i, :], x[:, bass.ds(first_tile + i, 1), :], scale[:, i:i + 1],
                                           rbias[:, i:i + 1], ALU.mult, ALU.add)
                op.then_inc(done, 1)

            def swap_halves():
                for i in range(4):
                    a, b = 32 * i, 32 * (i ^ 1)
                    op = dve.tensor_copy(swapped[a:a + 32, :], half[b:b + 32, :])
                link(op)

            def slot(g, s):
                has_next, has_ffn1, has_ffn2 = attends(s + 1), attends(s + 2), attends(s - 1)
                cur, nxt = s % 2, (s + 1) % 2

                def prepare_ffn(layer, gg):
                    if not (has_ffn1 if layer == 0 else has_ffn2):
                        return
                    if layer == 0:
                        if s < 1:
                            dve.wait_ge((s_load0, s_load1, s_loadrest)[s + 2], 16)
                    else:
                        dve.wait_ge(s_outadd, 4 * gg + 4)
                    statistics(TILES * gg)
                    normalise(y[layer], ry, TILES * gg, s_y[layer])

                def mix(layer, gg):
                    if not (has_ffn1 if layer == 0 else has_ffn2):
                        return
                    dve.wait_ge(s_yT[layer], gg + 1)
                    now, before = yT[layer][:, :, 1:], yT[layer][:, :, 0:SEQ]
                    diff = xk[layer][:, :].rearrange("p (b n) -> p b n", b=2)
                    link(dve.tensor_tensor(diff, now, before, ALU.subtract))
                    dve.scalar_tensor_tensor(xr[layer][:, :].rearrange("p (b n) -> p b n", b=2), diff,
                                             mu[:, 0:1], before, ALU.mult, ALU.add)
                    dve.scalar_tensor_tensor(diff, diff, mu[:, 1:2], before, ALU.mult, ALU.add).then_inc(s_mix[layer], 1)

                def double():
                    if has_ffn1:
                        dve.wait_ge(s_zT, g + 3)
                        at_block = zT[cur][:, :]
                        for i in range(2):
                            tokens = at_block[:, 32 * i:32 * i + GROUP].rearrange("p (b q) -> p b q", q=32)
                            for a in range(2):
                                dve.tensor_copy(keys_twice[:, :, a, 32 * i:32 * i + 32], tokens)
                        own = at_block[:, 32:].rearrange("p (b q) -> p b q", q=32)
                        dve.tensor_copy(queries_twice[:, :, :, :], own.unsqueeze(2).to_broadcast([128, BLOCKS, 2, 32])
                                        ).then_inc(s_twice, 1)

                def gated(layer, gg):
                    if not (has_ffn1 if layer == 0 else has_ffn2):
                        return
                    dve.wait_ge(s_th[layer], gg + 1)
                    dve.wait_ge(s_vp[layer], gg + 1)
                    dve.scalar_tensor_tensor(tanh_r[layer][:, :], tanh_r[layer][:, :], 1.0, wbank, ALU.add,
                                             ALU.mult).then_inc(s_gv[layer], 1)

                def prepare_z():
                    if not has_ffn1:
                        return
                    gg = g + 2
                    dve.wait_ge(s_x[0], gg + 1)
                    statistics(TILES * gg)
                    link(dve.tensor_copy(rscale[:, :], ry[:, :]))
                    link(dve.tensor_tensor(rt[:, :], rscale[:, :], rscale[:, :], ALU.mult))
                    link(dve.scalar_tensor_tensor(ra[:, :], mean_var[:, :, 1], float(DIM), rt[:, :], ALU.mult, ALU.mult))
                    link(dve.tensor_scalar(ra[:, :], ra[:, :], 1e-24, None, ALU.max))
                    reciprocal_root()
                    link(dve.scalar_tensor_tensor(rscale[:, :], rscale[:, :], float(DIM) ** 0.5, ry[:, :],
                                                  ALU.mult, ALU.mult))
                    normalise(z, rscale, TILES * gg, s_z)

                def zk(j):
                    if has_next:
                        dve.wait_ge(s_zkhi, 4 * (g + 1) + j + 1)
                        dve.tensor_tensor(zk_lo[nxt][:, 4 * j:4 * j + 4, :], wbank.rearrange("p (b c) -> p b c", c=128),
                                          zk_hi[nxt][:, 4 * j:4 * j + 4, :], ALU.subtract).then_inc(s_zklo, 1)

                def gates():
                    if has_next:
                        dve.wait_ge(s_gp, g + 2)
                        dve.tensor_tensor(gate[nxt][:, :, :], wbank[:, 0:128].rearrange("p (a h) -> p a h", h=HEADS),
                                          gate_bias[:, :].unsqueeze(1).to_broadcast([128, 8, HEADS]),
                                          ALU.add).then_inc(s_g, 1)

                def add_output(first_tile, quad):
                    dve.wait_ge(s_out, quad + 1)
                    dve.tensor_tensor(x[:, bass.ds(first_tile, 1), :], x[:, bass.ds(first_tile, 1), :],
                                      obank.unsqueeze(1), ALU.add).then_inc(s_outadd, 1)

                before_den = [[lambda: zk(0), lambda: zk(1)],
                              [lambda: mix(0, g + 2), lambda: mix(1, g - 1)],
                              [],
                              [prepare_z]]
                after_den = [[lambda: zk(2), lambda: zk(3), lambda: prepare_ffn(0, g + 2), lambda: prepare_ffn(1, g - 1)],
                             [gates],
                             [lambda: gated(0, g + 2)],
                             [lambda: gated(1, g - 1), double]]
                for q in range(QUADS):
                    quad = QUADS * g + q
                    if attends(s):
                        dve.wait_ge(s_factor, quad + 1)
                        link(dve.tensor_tensor(P[:, :], P[:, :], S[q % 2].rearrange("p a n -> p (a n)"), ALU.mult))
                        pairs = P[:, :].rearrange("p (a n) -> p a n", a=2)
                        dve.tensor_copy(P_even[0:64], pairs[0:64])
                        link(dve.tensor_copy(P_odd[64:128], pairs[64:128]))
                        dve.tensor_tensor(P_even[64:128], pairs[0:64], P_even[0:64], ALU.subtract)
                        dve.tensor_tensor(P_odd[0:64], pairs[64:128], P_odd[64:128], ALU.subtract).then_inc(s_p2, 1)
                    if exists(s, q):
                        dve.wait_ge(s_scores, quad + 2)
                        link(dve.tensor_reduce(half[:, :], S[(q + 1) % 2].rearrange("p a (h n) -> p (a h) n", n=32),
                                               AX.X, ALU.max, apply_transpose=True))
                        swap_halves()
                        link(dve.tensor_tensor(m_full[:, :], half[:, :], swapped[:, :], ALU.max))
                        link(dve.tensor_copy(m_hi[:, :], m_full[:, :]))
                        dve.scalar_tensor_tensor(m_parts[:, :], m_hi[:, :], minus_low[:, 0:1], m_full[:, :],
                                                 ALU.mult, ALU.add).then_inc(s_m, 1)
                    if attends(s) and q > 0:
                        add_output(TILES * g + q - 1, quad - 1)
                    if attends(s - 1) and q == 0:
                        add_output(TILES * g - 1, quad - 1)
                    for task in before_den[q]:
                        task()
                    if exists(s, q):
                        dve.wait_ge(s_exp, quad + 2)
                        own = cur if q < 3 else nxt
                        nq = (q + 1) % 4
                        if q == 3:
                            dve.wait_ge(s_gexp, g + 2)
                        link(dve.tensor_reduce(half[:, :], P[:, :].rearrange("p (a n) -> p a n", n=32),
                                               AX.X, ALU.add, apply_transpose=True))
                        swap_halves()
                        link(dve.tensor_tensor(den[:, :], half[:, :], swapped[:, :], ALU.add))
                        link(dve.scalar_tensor_tensor(den[:, :], gate[own][:, 2 * nq:2 * nq + 2, :].rearrange("p a h -> p (a h)"),
                                                      1.0, den[:, :], ALU.add, ALU.mult))
                        link(dve.reciprocal(f_full[:, :], den[:, :]))
                        link(dve.tensor_copy(f_hi[:, :], f_full[:, :]))
                        dve.scalar_tensor_tensor(f_parts[:, :], f_hi[:, :].bitcast(f32), minus_low[:, 0:1], f_full[:, :],
                                                 ALU.mult, ALU.add).then_inc(s_f, 1)
                    for task in after_den[q]:
                        task()

            for s in (-2, -1, 0, 1):
                slot(s, s)
            base = links[0]
            links[0] = 0
            with dve.Fori(0, 6) as it:
                links[1] = it * LINKS + base
                for k in range(2):
                    slot(it * 2 + (2 + k), 2 + k)
            assert links[0] == LINKS, links[0]
            links[0], links[1] = base + 6 * LINKS, 0
            for s in (14, 15, 16):
                slot(s, s)

        @block.gpsimd
        def _(pool):
            pool.wait_ge(s_const, 16)

            def diagonal(dst, parts, done):
                for i in range(2):
                    op = pool.tensor_tensor(dst[:, i, :].rearrange("p (h q) -> p h q", q=32),
                                            eye.unsqueeze(1).to_broadcast([128, HEADS, 32]),
                                            parts[:, 16 * i:16 * i + 16].unsqueeze(2).to_broadcast([128, HEADS, 32]),
                                            ALU.mult)
                op.then_inc(done, 1)

            def slot(g, s):
                has_ffn1, has_ffn2 = attends(s + 2), attends(s - 1)

                def square(layer, gg):
                    if has_ffn1 if layer == 0 else has_ffn2:
                        pool.wait_ge(s_relu[layer], gg + 1)
                        pool.tensor_tensor(kact[layer][:, :], kact[layer][:, :], kact[layer][:, :],
                                           ALU.mult).then_inc(s_kact[layer], 1)

                def add(layer, gg):
                    if has_ffn1 if layer == 0 else has_ffn2:
                        pool.wait_ge(s_gv[layer], gg + 1)
                        rows = x[:, bass.ds(TILES * gg, TILES), :]
                        pool.tensor_tensor(rows, rows, tanh_r[layer][:, :].rearrange("p (n c) -> p n c", c=DIM),
                                           ALU.add).then_inc(s_x[layer], 1)

                for q in range(QUADS):
                    quad = QUADS * g + q
                    if exists(s, q):
                        pool.wait_ge(s_m, quad + 2)
                        diagonal(shift_rows, m_parts, s_shiftrows)
                        pool.wait_ge(s_f, quad + 2)
                        diagonal(factor_rows, f_parts, s_factorrows)
                    if q == 1:
                        square(0, g + 2)
                    if q == 2:
                        add(0, g + 2)
                        square(1, g - 1)
                    if q == 3:
                        add(1, g - 1)

            loop_slots(pool, slot)


LINKS = 238


_INS = ['L0_attn_x', 'L0_attn_gamma', 'L0_attn_W_qkv', 'L0_attn_W_gates', 'L0_attn_b_gates', 'L0_attn_W_out',
        'L0_ffn_W_r', 'L0_ffn_W_k', 'L0_ffn_W_v', 'L0_ffn_mu_r', 'L0_ffn_mu_k']


def kernel(**inputs):
    import numpy as _np
    import concourse.bacc as _bacc
    from concourse import mybir as _mybir
    from concourse.bass_utils import run_bass_kernel_spmd as _run

    nc = _bacc.Bacc("TRN2", target_bir_lowering=False, num_devices=1)
    arrays, args = {}, []
    named = [(n, _np.ascontiguousarray(inputs[n])) for n in _INS] + [("constants", constants())]
    for name, a in named:
        arrays[f"in_{name}_dram"] = a
        args.append(nc.dram_tensor(f"in_{name}_dram", a.shape, _mybir.dt.from_np(a.dtype), kind="ExternalInput").ap())
    args.append(nc.dram_tensor("out_0_dram", (32, 256, 128), _mybir.dt.float32, kind="ExternalOutput").ap())
    macaron(nc, *args)
    r = _run(nc, [arrays], core_ids=[0])
    return r.results[0]["out_0_dram"]
```

```python
import numpy as np
import concourse.bass as bass
from concourse import mybir
from contextlib import ExitStack

TOKENS, DIM, HEADS, HEAD_DIM = 8192, 128, 16, 64
SEQ, WINDOW = 256, 32
GROUP = 512
GROUPS = TOKENS // GROUP
TILES = GROUP // 128
BLOCKS = GROUP // WINDOW
QUADS = BLOCKS // 4
LOOPS = (GROUPS - 6) // 2
HQ = HEADS * WINDOW
EPS = 1e-5
NEG = -1e30
T_HEADS = [range(0, 6), range(6, 11), range(11, 16), range(0)]
C_IDENT, C_EYE, C_MASK, C_BLOCK, C_LOW, C_END = 0, 128, 160, 224, 352, 353


def constants():
    p = np.arange(128)
    c = np.zeros((128, C_END), np.float32)
    c[:, C_IDENT:C_IDENT + 128] = np.eye(128)
    c[:, C_EYE:C_EYE + 32] = (p[:, None] % 32) == np.arange(32)[None]
    key, query = p[:, None] % 64, np.arange(32)[None]
    seen = (key >= query) & (key <= query + WINDOW)
    c[:, C_MASK:C_MASK + 32] = np.where(seen, 0.0, NEG)
    c[:, C_MASK + 32:C_MASK + 64] = np.where(seen & ((p[:, None] >= 64) | (key >= 32)), 0.0, NEG)
    c[:, C_BLOCK:C_BLOCK + 128] = (p[:, None] // 64) == (p[None] // 64)
    c[:, C_LOW] = (p // 32) % 2
    return c


def macaron(nc, x_in, gamma, w_qkv, w_gates, b_gates, w_out, w_r, w_k, w_v, mu_r, mu_k, consts, out):
    dt = mybir.dt
    f32, f32r, bf16, f16, i32 = dt.float32, dt.float32r, dt.bfloat16, dt.float16, dt.int32
    ALU, ACT, AX = mybir.AluOpType, mybir.ActivationFunctionType, mybir.AxisListType

    x_tiles = x_in.rearrange("b (n p) c -> p (b n) c", p=128)
    out_tiles = out.rearrange("b (n p) c -> p (b n) c", p=128)

    ctx = ExitStack()
    with ctx:
        def sb(name, shape, dtype=f32):
            return ctx.enter_context(nc.sbuf_tensor(name, shape, dtype))

        def sem(name):
            return ctx.enter_context(nc.semaphore(name))

        cst = sb("cst", [128, C_END])
        ident = cst[:, C_IDENT:C_IDENT + 128]
        eye = cst[:, C_EYE:C_EYE + 32]
        ident_bf = sb("ident_bf", [128, 128], bf16)
        mask_bf = sb("mask_bf", [128, 2, 32], bf16)
        minus_bf = sb("minus_bf", [128, 128], bf16)
        ones_r = sb("ones_r", [128, 128], f32r)
        minus_low = sb("minus_low", [128, 1])
        gam = sb("gam", [128, 1])
        mu = sb("mu", [128, 2])
        gate_bias = sb("gate_bias", [128, HEADS])
        wg = sb("wg", [128, HEADS])
        fold_qk = [sb(n, [128, HEADS, 128], f32r) for n in ("fold_qk_hi", "fold_qk_lo")]
        fold_vo = sb("fold_vo", [128, HEADS, 128])
        ffn_wT = sb("ffn_wT", [128, 3, 128])
        x = sb("x", [128, TOKENS // 128, DIM])
        t = [sb(f"t{i}", [128, HEADS, GROUP]) for i in range(2)]
        zT = [sb(f"zT{i}", [128, WINDOW + GROUP]) for i in range(2)]
        zk = [sb(f"zk{i}", [128, BLOCKS, 2, DIM], f16) for i in range(2)]
        zT_hi = sb("zT_hi", [128, GROUP], f32r)
        zT_lo = sb("zT_lo", [128, GROUP], f32r)
        z_parts = sb("z_parts", [128, TILES, 2, DIM], f16)
        gate_rows = sb("gate_rows", [128, TILES, HEADS])
        U = sb("U", [128, HEADS, 4, WINDOW])
        z = sb("z", [128, TILES, DIM])
        P = [sb(f"P{i}", [128, 2 * HQ]) for i in range(2)]
        P_even = sb("P_even", [128, 2, HQ], f16)
        P_odd = sb("P_odd", [128, 2, HQ], f16)
        shift_rows = sb("shift_rows", [128, 2, HQ], bf16)
        factor_rows = sb("factor_rows", [128, 2, HQ], f32r)
        half = sb("half", [128, 32])
        swapped = sb("swapped", [128, 32])
        m_full = sb("m_full", [128, 32])
        m_hi = sb("m_hi", [128, 32], bf16)
        m_parts = sb("m_parts", [128, 32], bf16)
        den = sb("den", [128, 32])
        f_full = sb("f_full", [128, 32])
        f_hi = sb("f_hi", [128, 32], f32r)
        f_parts = sb("f_parts", [128, 32])
        gate = [sb(f"gate{i}", [128, 8, HEADS]) for i in range(2)]
        stats = sb("stats", [128, TILES, 6])
        mean_var = sb("mean_var", [128, TILES, 2])
        ra, rt = (sb(n, [128, TILES]) for n in ("ra", "rt"))
        nscale, nbias = (sb(n, [128, 3, TILES]) for n in ("nscale", "nbias"))
        pause = sb("pause", [128, 1])
        act_pause = sb("act_pause", [128, 1])
        pool_pause = sb("pool_pause", [128, 1])
        y = [sb(f"y{i}", [128, TILES, DIM]) for i in range(2)]
        yT = [sb(f"yT{i}", [128, 2, SEQ + 1]) for i in range(2)]
        xr = [sb(f"xr{i}", [128, GROUP]) for i in range(2)]
        xk = [sb(f"xk{i}", [128, GROUP]) for i in range(2)]
        kact = [sb(f"kact{i}", [128, GROUP]) for i in range(2)]
        tanh_r = [sb(f"tanh_r{i}", [128, GROUP]) for i in range(2)]
        stage = t[1][:, :, :].rearrange("p h n -> p (h n)")
        wqkv_st = stage[:, 0:3072]
        wT_st = stage[:, 3072:6144].rearrange("p (j c) -> p j c", c=128)
        wout_st = stage[:, 6144:7168].rearrange("p (j c) -> p j c", c=128)
        ffn_st = stage[:, 7168:7552].rearrange("p (j c) -> p j c", c=128)

        ps = ctx.enter_context(nc.psum_tensor("ps", [128, 8, 512], f32))
        S = [ps[:, 0:2, :], ps[:, 2:4, :]]
        prod = [ps[:, 4 + i, :] for i in range(3)]
        wbank = ps[:, 7, :]
        obank = wbank[:, 0:128]

        s_const, s_weights, s_load0, s_load1, s_loadrest = (sem(n) for n in ("s_const", "s_weights", "s_load0", "s_load1", "s_loadrest"))
        s_prep, s_scaled, s_tr, s_trc, s_fold, s_set = (sem(n) for n in ("s_prep", "s_scaled", "s_tr", "s_trc", "s_fold", "s_set"))
        s_pad = sem("s_pad")
        s_scores, s_m, s_shiftrows, s_shift, s_exp = (sem(n) for n in ("s_scores", "s_m", "s_shiftrows", "s_shift", "s_exp"))
        s_f, s_factorrows, s_factor, s_scaled_p = (sem(n) for n in ("s_f", "s_factorrows", "s_factor", "s_scaled_p"))
        s_phi, s_plo_even, s_plo_odd = (sem(n) for n in ("s_phi", "s_plo_even", "s_plo_odd"))
        s_prod, s_evac, s_out, s_outadd = (sem(n) for n in ("s_prod", "s_evac", "s_out", "s_outadd"))
        s_z, s_zTp, s_zT, s_zTlo, s_zhi, s_zlo, s_zk = (
            sem(n) for n in ("s_z", "s_zTp", "s_zT", "s_zTlo", "s_zhi", "s_zlo", "s_zk"))
        s_gp, s_g, s_gexp, s_gate = (sem(n) for n in ("s_gp", "s_g", "s_gexp", "s_gate"))
        s_zstat = sem("s_zstat")
        s_stat, s_diff, s_y, s_yTp, s_yT, s_mix, s_kp, s_relu, s_kact, s_rp, s_th, s_vp, s_gv, s_x = (
            [sem(f"{n}{i + 1}") for i in range(2)]
            for n in ("s_stat", "s_diff", "s_y", "s_yTp", "s_yT", "s_mix", "s_kp", "s_relu", "s_kact", "s_rp", "s_th", "s_vp", "s_gv", "s_x"))
        s_link, s_store = sem("s_link"), sem("s_store")

        def attends(s):
            return 0 <= s < GROUPS

        def exists(s, q):
            return 0 <= QUADS * s + q + 1 < QUADS * GROUPS

        def products_before(g, s):
            if s < 0:
                return 0
            return HEADS * (s < GROUPS) + (HEADS + BLOCKS) * g

        def has_before(s, q):
            return 0 <= QUADS * s + q - 1 < QUADS * GROUPS

        def loop_slots(engine, slot):
            for s in (-2, -1, 0, 1):
                slot(s, s)
            with engine.Fori(0, LOOPS) as it:
                for k in range(2):
                    slot(it * 2 + (2 + k), 2 + k)
            for s in range(2 + 2 * LOOPS, GROUPS + 1):
                slot(s, s)

        def fold_heads(dst, odd, hb):
            return dst[:, 8 * hb + odd:8 * hb + odd + 7:2, :]

        def fold_bank(k, odd, hb):
            return ps[:, 4 * k + 2 * odd + hb, :].rearrange("p (j c) -> p j c", c=128)

        block = ctx.enter_context(nc.Block())

        @block.sync
        def _(sp):
            sp.dma_start(cst[:, :], consts).then_inc(s_const, 16)
            sp.dma_start(wqkv_st, w_qkv).then_inc(s_weights, 16)
            sp.dma_start(wout_st, w_out.rearrange("(j p) c -> p j c", p=128)).then_inc(s_weights, 16)
            sp.dma_start(x[:, 0:TILES, :], x_tiles[:, 0:TILES, :]).then_inc(s_load0, 16)
            sp.dma_start(x[:, TILES:2 * TILES, :], x_tiles[:, TILES:2 * TILES, :]).then_inc(s_load1, 16)
            sp.dma_start(x[:, 2 * TILES:, :], x_tiles[:, 2 * TILES:, :]).then_inc(s_loadrest, 16)

            def slot(g, s):
                cur = s % 2
                if attends(s + 2):
                    sp.wait_ge(s_zhi, g + 3)
                    sp.wait_ge(s_zlo, g + 3)
                    if s >= 0:
                        sp.wait_ge(s_evac, products_before(g + 1, s + 1))
                    for j in range(4):
                        src = z_parts[32 * j:32 * j + 32, :, :, :]
                        for a in range(2):
                            sp.dma_start(zk[cur][64 * a + 32:64 * a + 64, j:BLOCKS:4, :, :], src).then_inc(s_zk, 16)
                            n = TILES if j < 3 else TILES - 1
                            sp.dma_start(zk[cur][64 * a:64 * a + 32, j + 1:BLOCKS:4, :, :], src[:, 0:n]).then_inc(s_zk, 16)
                    sp.wait_ge(s_gexp, g + 3)
                    for j in range(4):
                        for a in range(2):
                            d = 64 * (j % 2) + 32 * a
                            sp.dma_start(gate[cur][d:d + 32, j // 2:8:2, :], gate_rows[32 * j:32 * j + 32, :, :]
                                         ).then_inc(s_gate, 16)
                if attends(s - 1):
                    sp.wait_ge(s_x[1], g)
                    rows = bass.ds(TILES * (g - 1), TILES)
                    sp.dma_start(out_tiles[:, rows, :], x[:, rows, :]).then_inc(s_store, 16)

            loop_slots(sp, slot)
            sp.wait_ge(s_store, 16 * GROUPS)

        @block.tensor
        def _(pe):
            mm = pe.matmul
            pe.wait_ge(s_const, 16)
            pe.wait_ge(s_prep, 1)
            for j in range(3):
                i = pe.transpose(wbank[:, 128 * j:128 * j + 128], ffn_st[:, j, :], ident)
            i.then_inc(s_tr, 1)
            pe.wait_ge(s_scaled, 1)
            for b in range(6):
                for j in range(4):
                    c = 128 * (4 * b + j)
                    i = pe.transpose(ps[:, b, 128 * j:128 * j + 128], wqkv_st[:, c:c + 128], ident)
                i.then_inc(s_tr, 1)
            pe.wait_ge(s_trc, 7)
            for k, (a, b) in enumerate(((lambda j: wT_st[:, j, :], lambda j: wT_st[:, 8 + j, :]),
                                        (lambda j: wT_st[:, 16 + j, :], lambda j: wout_st[:, j, :]))):
                for h in range(HEADS):
                    j, r = h // 2, (h % 2) * 64
                    bank, col = 4 * k + 2 * (h % 2) + j // 4, 128 * (j % 4)
                    i = mm(ps[:, bank, col:col + 128], a(j)[r:r + 64, :], b(j)[r:r + 64, :], start=True, stop=True)
                i.then_inc(s_fold, 1)
            pe.wait_ge(s_set, 3)

            release = [None]

            def take_work_bank():
                if release[0] is not None:
                    pe.wait_ge(*release[0])

            def work_transposes(src, done, value, freed, made, made_value):
                pe.wait_ge(made, made_value)
                take_work_bank()
                for i in range(TILES):
                    op = pe.transpose(wbank[:, 128 * i:128 * i + 128], src[:, i, :], ident)
                op.then_inc(done, 1)
                release[0] = (freed, value)

            def slot(g, s):
                has_next, has_ffn1, has_ffn2 = attends(s + 1), attends(s + 2), attends(s - 1)
                cur, nxt = s % 2, (s + 1) % 2
                if s > -2:
                    release[0] = (s_g, g + 2) if has_next else (s_gv[1], g - 1)
                count = [0, 0]

                def product():
                    if count[1] >= 3:
                        pe.wait_ge(s_evac, products_before(g, s) + count[0] - 2)
                    bank = prod[count[1] % 3]
                    count[0] += 1
                    count[1] += 1
                    return bank

                def gates():
                    if not has_ffn1:
                        return
                    pe.wait_ge(s_zT, g + 3)
                    take_work_bank()
                    for i in range(TILES):
                        tokens = zT[cur][:, WINDOW + 128 * i:WINDOW + 128 * i + 128]
                        op = mm(wbank[:, 16 * i:16 * i + 16], tokens, wg[:, :], start=True, stop=True)
                        if i < TILES - 1:
                            yield
                    op.then_inc(s_gp, 1)
                    release[0] = (s_g, g + 3)
                    yield

                def ffn(layer, gg, stage_):
                    if not (has_ffn1 if layer == 0 else has_ffn2):
                        return
                    if stage_[0] == "T":
                        return work_transposes(y[layer], s_yTp[layer], gg + 1, s_yT[layer], s_y[layer], gg + 1)
                    if stage_ == "k":
                        pe.wait_ge(s_mix[layer], gg + 1)
                        take_work_bank()
                        mm(wbank, ffn_wT[:, 1, :], xk[layer][:, :], start=True, stop=True).then_inc(s_kp[layer], 1)
                        release[0] = (s_relu[layer], gg + 1)
                    if stage_ == "r":
                        take_work_bank()
                        for i in range(TILES):
                            c = slice(128 * i, 128 * i + 128)
                            op = mm(wbank[:, c], xr[layer][:, c], ffn_wT[:, 0, :], start=True, stop=True)
                        op.then_inc(s_rp[layer], 1)
                        release[0] = (s_th[layer], gg + 1)
                    if stage_ == "v":
                        pe.wait_ge(s_kact[layer], gg + 1)
                        take_work_bank()
                        for i in range(TILES):
                            c = slice(128 * i, 128 * i + 128)
                            op = mm(wbank[:, c], kact[layer][:, c], ffn_wT[:, 2, :], start=True, stop=True)
                        op.then_inc(s_vp[layer], 1)
                        release[0] = (s_gv[layer], gg + 1)

                def z_transposes():
                    if has_ffn1:
                        work_transposes(z, s_zTp, g + 3, s_zT, s_z, g + 3)

                work = [{"early": lambda: ffn(0, g + 2, "T"), "last": lambda: ffn(0, g + 2, "k")},
                        {"early": lambda: ffn(0, g + 2, "r"), "late": lambda: ffn(0, g + 2, "v"),
                         "last": lambda: ffn(1, g - 1, "T")},
                        {"late": lambda: ffn(1, g - 1, "k"), "last": lambda: ffn(1, g - 1, "r")},
                        {"late": z_transposes, "within": lambda: ffn(1, g - 1, "v")}]

                def do(q, when):
                    if when in work[q]:
                        work[q][when]()

                for q in range(QUADS):
                    quad = QUADS * g + q
                    new = exists(s, q)
                    nq, par = (q + 1) % 4, (q + 1) % 2
                    own = cur if q < 3 else nxt
                    if new:
                        for i in range(2):
                            first = nq % 2 == 0 and i == 0
                            band = mask_bf[:, int(first), :].unsqueeze(1).to_broadcast([128, HEADS, 32])
                            mm(S[par][:, i, :], ident_bf[:, :], band, start=True, stop=False, skip_group_check=True)
                        if q == 3:
                            pe.wait_ge(s_evac, products_before(g, s) + count[0] - 4 * attends(s))
                        for i in range(2):
                            for j in range(2):
                                b = 4 * nq + 2 * i + j
                                op = mm(S[par][64 * j:64 * j + 64, i, :], zT[own][:, 32 * b:32 * b + 64],
                                        t[own][:, :, 32 * b:32 * b + 32], start=False, stop=True, skip_group_check=True)
                        op.then_inc(s_scores, 1)
                    do(q, "early")
                    if attends(s):
                        for i in range(2):
                            pe.wait_ge(s_factorrows, 2 * quad + 1 + i)
                            op = mm(S[q % 2][:, i, :], ones_r[:, :], factor_rows[:, i, :], start=True, stop=True)
                        op.then_inc(s_factor, 1)
                    count[1] = 0
                    if s >= 0 or count[0]:
                        pe.wait_ge(s_evac, products_before(g, s) + count[0])
                    if has_before(s, q):
                        take_work_bank()
                        for h in range(HEADS):
                            op = mm(obank, U[:, h, :, :].rearrange("p b q -> p (b q)"), fold_vo[:, h, :],
                                    start=(h == 0), stop=(h == HEADS - 1))
                        op.then_inc(s_out, 1)
                        release[0] = (s_outadd, quad)
                    if new:
                        for i in range(2):
                            pe.wait_ge(s_shiftrows, 2 * quad + 3 + i)
                            op = mm(S[par][:, i, :], minus_bf[:, :], shift_rows[:, i, :], start=False, stop=True,
                                    skip_group_check=True)
                        op.then_inc(s_shift, 1)
                    if has_next:
                        if q == 0:
                            pe.wait_ge(s_zTlo, g + 2)
                        for h in T_HEADS[q]:
                            bank = product()
                            mm(bank, fold_qk[1][:, h, :], zT_hi[:, :], start=True, stop=False)
                            mm(bank, fold_qk[0][:, h, :], zT_lo[:, :], start=False, stop=False)
                            mm(bank, fold_qk[0][:, h, :], zT_hi[:, :], start=False, stop=True).then_inc(s_prod, 1)
                    do(q, "late")
                    if attends(s):
                        if q == 0:
                            pe.wait_ge(s_zk, 256 * (g + 1))
                        pe.wait_ge(s_plo_even, quad + 1)
                        pe.wait_ge(s_plo_odd, quad + 1)
                        gate_products = gates() if q == 3 else iter(())
                        for b in range(4):
                            bank = product()
                            probs = (P_odd if b % 2 else P_even)[:, b // 2, :]
                            mm(bank, zk[cur][:, 4 * q + b, 0, :], probs, start=True, stop=False)
                            if b >= 2:
                                next(gate_products, None)
                            mm(bank, zk[cur][:, 4 * q + b, 1, :], probs, start=False, stop=True).then_inc(s_prod, 1)
                            if b == 0:
                                do(q, "within")
                            if b >= 2:
                                next(gate_products, None)
                    else:
                        do(q, "within")
                        if q == 3:
                            for _ in gates():
                                pass
                    do(q, "last")

            loop_slots(pe, slot)

        @block.scalar
        def _(act):
            def wait(sem_, value):
                act.wait_ge(sem_, value)
                act.wait_ge(s_const, 16)

            act.dma_start(ffn_st[:, 0, :], w_r).then_inc(s_weights, 16)
            act.dma_start(ffn_st[:, 1, :], w_k).then_inc(s_weights, 16)
            act.dma_start(ffn_st[:, 2, :], w_v).then_inc(s_weights, 16)
            act.dma_start(gam[:, :], gamma.rearrange("(p a) -> p a", a=1)).then_inc(s_weights, 16)
            act.dma_start(mu[:, 0:1], mu_r.rearrange("(p a) -> p a", a=1)).then_inc(s_weights, 16)
            act.dma_start(mu[:, 1:2], mu_k.rearrange("(p a) -> p a", a=1)).then_inc(s_weights, 16)
            act.dma_start(wg[:, :], w_gates).then_inc(s_weights, 16)
            act.dma_start(gate_bias[:, :], b_gates.rearrange("(a h) -> a h", a=1).partition_broadcast(128)
                          if False else b_gates.rearrange("(a h) -> a h", a=1).to_broadcast([128, HEADS])).then_inc(s_weights, 16)
            act.wait_ge(s_tr, 1)
            act.activation(ffn_wT[:, 0:2, :], wbank[:, 0:256].rearrange("p (j c) -> p j c", c=128), ACT.Copy)
            act.activation(ffn_wT[:, 2, :], wbank[:, 256:384], ACT.Copy, scale=0.25).then_inc(s_trc, 1)
            for b in range(6):
                act.wait_ge(s_tr, b + 2)
                act.activation(wT_st[:, 4 * b:4 * b + 4, :], ps[:, b, :].rearrange("p (j c) -> p j c", c=128),
                               ACT.Copy, scale=HEAD_DIM ** -0.5 if b < 2 else 1.0).then_inc(s_trc, 1)
            for k, dst in enumerate((fold_qk[0], fold_vo)):
                act.wait_ge(s_fold, k + 1)
                for odd in range(2):
                    for hb in range(2):
                        op = act.activation(fold_heads(dst, odd, hb), fold_bank(k, odd, hb), ACT.Copy)
                op.then_inc(s_set, 1)
            act.wait_ge(s_pad, 1)

            def normalise(which, dst, gg, ready, done):
                wait(ready, gg + 1)
                act.activation(act_pause[:, :], cst[:, 0:1], ACT.Copy)
                for i in range(TILES):
                    rows = x[:, bass.ds(TILES * gg + i, 1), :]
                    op = act.activation(dst[:, i:i + 1, :], rows, ACT.Identity, scale=nscale[:, which, i:i + 1],
                                        bias=nbias[:, which, i:i + 1])
                op.then_inc(done, 1)

            def slot(g, s):
                has_next, has_ffn1, has_ffn2 = attends(s + 1), attends(s + 2), attends(s - 1)
                cur, nxt = s % 2, (s + 1) % 2
                count = [0, 0]

                def evacuate(dst, by_head=False):
                    n = products_before(g, s) + count[0]
                    wait(s_prod, n + 1)
                    src = prod[count[1] % 3]
                    if by_head:
                        src = src.rearrange("p (h q) -> p h q", q=WINDOW)
                    act.activation(dst, src, ACT.Copy).then_inc(s_evac, 1)
                    count[0] += 1
                    count[1] += 1

                def ffn(layer, gg, stage_):
                    if not (has_ffn1 if layer == 0 else has_ffn2):
                        return
                    if stage_[0] == "T":
                        wait(s_yTp[layer], gg + 1)
                        act.activation(yT[layer][:, :, 1:], wbank.rearrange("p (b n) -> p b n", b=2),
                                       ACT.Copy).then_inc(s_yT[layer], 1)
                    if stage_ == "k":
                        wait(s_kp[layer], gg + 1)
                        act.activation(kact[layer][:, :], wbank, ACT.Relu).then_inc(s_relu[layer], 1)
                    if stage_ == "r":
                        if s + (2 if layer == 0 else -1) > 0:
                            wait(s_x[layer], gg)
                        wait(s_rp[layer], gg + 1)
                        act.activation(tanh_r[layer][:, :], wbank, ACT.Tanh, scale=0.5).then_inc(s_th[layer], 1)

                def z_out():
                    if has_ffn1:
                        wait(s_zTp, g + 3)
                        act.activation(zT[cur][:, WINDOW:], wbank, ACT.Copy).then_inc(s_zT, 1)
                        if s > -2:
                            wait(s_zk, 256 * (g + 2))
                        act.activation(z_parts[:, :, 0, :], z[:, :, :], ACT.Copy).then_inc(s_zhi, 1)

                def gates():
                    if has_ffn1:
                        wait(s_g, g + 3)
                        act.activation(gate_rows[:, :, :], gate_rows[:, :, :], ACT.Exp, scale=-1.0).then_inc(s_gexp, 1)

                for q in range(QUADS):
                    quad = QUADS * g + q
                    count[1] = 0
                    if q == 0:
                        ffn(0, g + 2, "T")
                    if q == 1:
                        ffn(0, g + 2, "r")
                    if attends(s):
                        wait(s_scaled_p, quad + 1)
                        pairs = P[q % 2][:, :].rearrange("p (a n) -> p a n", a=2)
                        act.activation(P_odd[64:128], pairs[64:128], ACT.Copy).then_inc(s_phi, 1)
                        act.activation(P_even[0:64], pairs[0:64], ACT.Copy).then_inc(s_phi, 1)
                    if exists(s, q):
                        wait(s_shift, quad + 2)
                        act.activation(P[(q + 1) % 2][:, :], S[(q + 1) % 2].rearrange("p a n -> p (a n)"),
                                       ACT.Exp).then_inc(s_exp, 1)
                    if has_next:
                        if q == 0 and s > 0:
                            wait(s_scores, 4 * g)
                        for h in T_HEADS[q]:
                            evacuate(t[nxt][:, h, :])
                    if q == 1 and has_ffn2:
                        normalise(1, y[1], g - 1, s_stat[1], s_y[1])
                    if q == 2:
                        ffn(1, g - 1, "k")
                    if q == 3:
                        z_out()
                    if attends(s):
                        for b in range(4):
                            evacuate(U[:, :, b, :], True)
                    if q == 0:
                        ffn(0, g + 2, "k")
                    if q == 1:
                        ffn(1, g - 1, "T")
                    if q == 2:
                        ffn(1, g - 1, "r")
                        if has_ffn1:
                            normalise(2, z, g + 2, s_zstat, s_z)
                    if q == 3:
                        gates()
                        if attends(s + 3):
                            normalise(0, y[0], g + 3, s_stat[0], s_y[0])

            normalise(0, y[0], 0, s_stat[0], s_y[0])
            loop_slots(act, slot)

        @block.vector
        def _(dve):
            links = [0, 0]

            def link(op):
                links[0] += 1
                op.then_inc(s_link, 1)
                dve.wait_ge(s_link, links[0] + links[1])

            dve.memset(zT[0][:, 0:WINDOW], 0.0)
            dve.memset(zT[1][:, 0:WINDOW], 0.0)
            for i in range(2):
                dve.memset(zk[i][:, 0:1, :, :], 0.0)
            for i in range(2):
                op = dve.memset(yT[i][:, :, 0:1], 0.0)
            op.then_inc(s_pad, 1)
            dve.wait_ge(s_const, 16)
            dve.tensor_copy(ident_bf[:, :], ident)
            dve.tensor_copy(mask_bf[:, :, :], cst[:, C_MASK:C_MASK + 64].rearrange("p (k q) -> p k q", k=2))
            dve.tensor_scalar(minus_bf[:, :], cst[:, C_BLOCK:C_BLOCK + 128], -1.0, None, ALU.mult)
            dve.tensor_copy(ones_r[:, :], cst[:, C_BLOCK:C_BLOCK + 128])
            dve.tensor_scalar(minus_low[:, :], cst[:, C_LOW:C_LOW + 1], -1.0, None, ALU.mult)
            dve.wait_ge(s_weights, 16 * 10)
            link(dve.tensor_scalar(wg[:, :], wg[:, :], gam[:, 0:1], None, ALU.mult))
            dve.tensor_copy(rt[:, 0:1], gam[:, :]).then_inc(s_prep, 1)
            dve.tensor_scalar(wqkv_st, wqkv_st, gam[:, 0:1], None, ALU.mult).then_inc(s_scaled, 1)

            for odd in range(2):
                for hb in range(2):
                    if odd + hb == 0:
                        dve.wait_ge(s_set, 1)
                    op = dve.tensor_tensor(fold_heads(fold_qk[1], odd, hb), fold_bank(0, odd, hb),
                                           fold_heads(fold_qk[0], odd, hb).bitcast(f32), ALU.subtract)
            op.then_inc(s_set, 1)

            def statistics(first_tile, which, done):
                dve.memset(pause[:, :], 0.0)
                for i in range(TILES):
                    op = dve.bn_stats(stats[:, i, :], x[:, bass.ds(first_tile + i, 1), :])
                link(op)
                dve.memset(pause[:, :], 0.0)
                for i in range(TILES):
                    op = dve.bn_aggr(mean_var[:, i, :], stats[:, i, :])
                link(op)
                var, root, bias = mean_var[:, :, 1], nscale[:, which, :], nbias[:, which, :]
                if which == 2:
                    link(dve.tensor_scalar(ra[:, :], var, EPS, 1e-24 / DIM, ALU.add, ALU.mult))
                    link(dve.tensor_tensor(ra[:, :], var, ra[:, :], ALU.max))
                else:
                    link(dve.tensor_scalar(ra[:, :], var, EPS, None, ALU.add))
                link(dve.tensor_scalar(root.bitcast(i32), ra[:, :].bitcast(i32), -0.5, float(0x5F3759DF),
                                       ALU.mult, ALU.add))
                for _ in range(3):
                    link(dve.tensor_tensor(rt[:, :], root, root, ALU.mult))
                    link(dve.scalar_tensor_tensor(rt[:, :], rt[:, :], -0.5, ra[:, :], ALU.mult, ALU.mult))
                    link(dve.scalar_tensor_tensor(root, rt[:, :], 1.5, root, ALU.add, ALU.mult))
                dve.scalar_tensor_tensor(bias, mean_var[:, :, 0], -1.0, root, ALU.mult, ALU.mult).then_inc(done, 1)

            def swap_halves():
                for i in range(4):
                    a, b = 32 * i, 32 * (i ^ 1)
                    op = dve.tensor_copy(swapped[a:a + 32, :], half[b:b + 32, :])
                link(op)

            def slot(g, s):
                has_next, has_ffn1, has_ffn2 = attends(s + 1), attends(s + 2), attends(s - 1)
                cur, nxt = s % 2, (s + 1) % 2

                def prepare_first(s_, gg):
                    if attends(s_):
                        if s_ < 3:
                            dve.wait_ge((s_load0, s_load1, s_loadrest)[s_], 16)
                        statistics(TILES * gg, 0, s_stat[0])

                def prepare_second():
                    if has_ffn2:
                        dve.wait_ge(s_outadd, 4 * g)
                        statistics(TILES * (g - 1), 1, s_stat[1])

                def mix(layer, gg):
                    if not (has_ffn1 if layer == 0 else has_ffn2):
                        return
                    dve.wait_ge(s_diff[layer], gg + 1)
                    before = yT[layer][:, :, 0:SEQ]
                    diff = xk[layer][:, :].rearrange("p (b n) -> p b n", b=2)
                    dve.scalar_tensor_tensor(xr[layer][:, :].rearrange("p (b n) -> p b n", b=2), diff,
                                             mu[:, 0:1], before, ALU.mult, ALU.add)
                    dve.scalar_tensor_tensor(diff, diff, mu[:, 1:2], before, ALU.mult, ALU.add).then_inc(s_mix[layer], 1)

                def gated(layer, gg):
                    if not (has_ffn1 if layer == 0 else has_ffn2):
                        return
                    dve.wait_ge(s_th[layer], gg + 1)
                    dve.wait_ge(s_vp[layer], gg + 1)
                    dve.scalar_tensor_tensor(tanh_r[layer][:, :], tanh_r[layer][:, :], 1.0, wbank, ALU.add,
                                             ALU.mult).then_inc(s_gv[layer], 1)

                def prepare_z():
                    if has_ffn1:
                        dve.wait_ge(s_x[0], g + 3)
                        statistics(TILES * (g + 2), 2, s_zstat)

                def z_low():
                    if has_ffn1:
                        dve.wait_ge(s_zT, g + 3)
                        link(dve.tensor_copy(zT_hi[:, :], zT[cur][:, WINDOW:]))
                        dve.tensor_tensor(zT_lo[:, :], zT[cur][:, WINDOW:], zT_hi[:, :].bitcast(f32), ALU.subtract
                                          ).then_inc(s_zTlo, 1)
                        dve.wait_ge(s_zhi, g + 3)
                        dve.tensor_tensor(z_parts[:, :, 1, :], z[:, :, :], z_parts[:, :, 0, :], ALU.subtract
                                          ).then_inc(s_zlo, 1)

                def gates():
                    if has_ffn1:
                        dve.wait_ge(s_gp, g + 3)
                        if s > -2:
                            dve.wait_ge(s_gate, 128 * (g + 2))
                        dve.tensor_tensor(gate_rows[:, :, :], wbank[:, 0:64].rearrange("p (a h) -> p a h", h=HEADS),
                                          gate_bias[:, :].unsqueeze(1).to_broadcast([128, TILES, HEADS]),
                                          ALU.add).then_inc(s_g, 1)

                def add_output(first_tile, quad):
                    dve.wait_ge(s_out, quad + 1)
                    dve.tensor_tensor(x[:, bass.ds(first_tile, 1), :], x[:, bass.ds(first_tile, 1), :],
                                      obank.unsqueeze(1), ALU.add).then_inc(s_outadd, 1)

                after_mult = [[lambda: mix(0, g + 2)], [], [lambda: mix(1, g - 1)], []]
                before_den = [[], [], [], [z_low]]
                after_den = [[prepare_second],
                             [lambda: gated(0, g + 2), lambda: prepare_first(s + 3, g + 3)],
                             [prepare_z],
                             [lambda: gated(1, g - 1), gates]]
                if s == -2:
                    prepare_first(0, 0)
                for q in range(QUADS):
                    quad = QUADS * g + q
                    if exists(s, q):
                        dve.wait_ge(s_scores, quad + 2)
                        link(dve.tensor_reduce(half[:, :], S[(q + 1) % 2].rearrange("p a (h n) -> p (a h) n", n=32),
                                               AX.X, ALU.max, apply_transpose=True))
                        swap_halves()
                        link(dve.tensor_tensor(m_full[:, :], half[:, :], swapped[:, :], ALU.max))
                        link(dve.tensor_copy(m_hi[:, :], m_full[:, :]))
                        dve.scalar_tensor_tensor(m_parts[:, :], m_hi[:, :], minus_low[:, 0:1], m_full[:, :],
                                                 ALU.mult, ALU.add).then_inc(s_m, 1)
                    if attends(s):
                        dve.wait_ge(s_factor, quad + 1)
                        dve.tensor_tensor(P[q % 2][:, :], P[q % 2][:, :], S[q % 2].rearrange("p a n -> p (a n)"),
                                          ALU.mult).then_inc(s_scaled_p, 1)
                    if has_before(s, q):
                        add_output(TILES * g + q - 1, quad - 1)
                    for task in after_mult[q]:
                        task()
                    if attends(s):
                        dve.wait_ge(s_phi, 2 * quad + 2)
                        pairs = P[q % 2][:, :].rearrange("p (a n) -> p a n", a=2)
                        dve.tensor_tensor(P_even[64:128], pairs[0:64], P_even[0:64], ALU.subtract).then_inc(s_plo_even, 1)
                    for task in before_den[q]:
                        task()
                    if exists(s, q):
                        dve.wait_ge(s_exp, quad + 2)
                        own = cur if q < 3 else nxt
                        nq = (q + 1) % 4
                        if q == 3:
                            dve.wait_ge(s_gate, 128 * (g + 2))
                        link(dve.tensor_reduce(half[:, :], P[(q + 1) % 2][:, :].rearrange("p (a n) -> p a n", n=32),
                                               AX.X, ALU.add, apply_transpose=True))
                        swap_halves()
                        link(dve.tensor_tensor(den[:, :], half[:, :], swapped[:, :], ALU.add))
                        link(dve.scalar_tensor_tensor(den[:, :], gate[own][:, 2 * nq:2 * nq + 2, :].rearrange("p a h -> p (a h)"),
                                                      1.0, den[:, :], ALU.add, ALU.mult))
                        link(dve.reciprocal(f_full[:, :], den[:, :]))
                        link(dve.tensor_copy(f_hi[:, :], f_full[:, :]))
                        dve.scalar_tensor_tensor(f_parts[:, :], f_hi[:, :].bitcast(f32), minus_low[:, 0:1], f_full[:, :],
                                                 ALU.mult, ALU.add).then_inc(s_f, 1)
                    for task in after_den[q]:
                        task()

            for s in (-2, -1, 0, 1):
                slot(s, s)
            base = links[0]
            links[0] = 0
            with dve.Fori(0, LOOPS) as it:
                links[1] = it * LINKS + base
                for k in range(2):
                    slot(it * 2 + (2 + k), 2 + k)
            assert links[0] == LINKS, links[0]
            links[0], links[1] = base + LOOPS * LINKS, 0
            for s in range(2 + 2 * LOOPS, GROUPS + 1):
                slot(s, s)

        @block.gpsimd
        def _(pool):
            pool.wait_ge(s_const, 16)

            def diagonal(dst, parts, done):
                for i in range(2):
                    op = pool.tensor_tensor(dst[:, i, :].rearrange("p (h q) -> p h q", q=32),
                                            eye.unsqueeze(1).to_broadcast([128, HEADS, 32]),
                                            parts[:, 16 * i:16 * i + 16].unsqueeze(2).to_broadcast([128, HEADS, 32]),
                                            ALU.mult)
                    op.then_inc(done, 1)

            def slot(g, s):
                has_ffn1, has_ffn2 = attends(s + 2), attends(s - 1)

                def difference(layer, gg):
                    if has_ffn1 if layer == 0 else has_ffn2:
                        pool.wait_ge(s_yT[layer], gg + 1)
                        pool.tensor_tensor(xk[layer][:, :].rearrange("p (b n) -> p b n", b=2), yT[layer][:, :, 1:],
                                           yT[layer][:, :, 0:SEQ], ALU.subtract).then_inc(s_diff[layer], 1)

                def square(layer, gg):
                    if has_ffn1 if layer == 0 else has_ffn2:
                        pool.wait_ge(s_relu[layer], gg + 1)
                        pool.tensor_tensor(kact[layer][:, :], kact[layer][:, :], kact[layer][:, :],
                                           ALU.mult).then_inc(s_kact[layer], 1)

                def add(layer, gg):
                    if has_ffn1 if layer == 0 else has_ffn2:
                        pool.wait_ge(s_gv[layer], gg + 1)
                        pool.tensor_tensor(pool_pause[:, :], eye[:, 0:1], eye[:, 0:1], ALU.mult)
                        rows = x[:, bass.ds(TILES * gg, TILES), :]
                        pool.tensor_tensor(rows, rows, tanh_r[layer][:, :].rearrange("p (n c) -> p n c", c=DIM),
                                           ALU.add).then_inc(s_x[layer], 1)

                for q in range(QUADS):
                    quad = QUADS * g + q
                    if q == 0:
                        difference(0, g + 2)
                    if q == 1:
                        square(0, g + 2)
                    if q == 2:
                        difference(1, g - 1)
                    if q == 3:
                        square(1, g - 1)
                    if exists(s, q):
                        pool.wait_ge(s_m, quad + 2)
                        diagonal(shift_rows, m_parts, s_shiftrows)
                    if attends(s):
                        pool.drain()
                        pool.wait_ge(s_phi, 2 * quad + 1)
                        pairs = P[q % 2][:, :].rearrange("p (a n) -> p a n", a=2)
                        pool.tensor_tensor(P_odd[0:64], pairs[64:128], P_odd[64:128], ALU.subtract).then_inc(s_plo_odd, 1)
                        pool.wait_ge(s_plo_odd, quad + 1)
                    if exists(s, q):
                        pool.wait_ge(s_f, quad + 2)
                        diagonal(factor_rows, f_parts, s_factorrows)
                    if q == 1:
                        add(0, g + 2)
                    if q == 3:
                        add(1, g - 1)

            loop_slots(pool, slot)


LINKS = 162


_INS = ['L0_attn_x', 'L0_attn_gamma', 'L0_attn_W_qkv', 'L0_attn_W_gates', 'L0_attn_b_gates', 'L0_attn_W_out',
        'L0_ffn_W_r', 'L0_ffn_W_k', 'L0_ffn_W_v', 'L0_ffn_mu_r', 'L0_ffn_mu_k']


def kernel(**inputs):
    import numpy as _np
    import concourse.bacc as _bacc
    from concourse import mybir as _mybir
    from concourse.bass_utils import run_bass_kernel_spmd as _run

    nc = _bacc.Bacc("TRN2", target_bir_lowering=False, num_devices=1)
    arrays, args = {}, []
    named = [(n, _np.ascontiguousarray(inputs[n])) for n in _INS] + [("constants", constants())]
    for name, a in named:
        arrays[f"in_{name}_dram"] = a
        args.append(nc.dram_tensor(f"in_{name}_dram", a.shape, _mybir.dt.from_np(a.dtype), kind="ExternalInput").ap())
    args.append(nc.dram_tensor("out_0_dram", (32, 256, 128), _mybir.dt.float32, kind="ExternalOutput").ap())
    macaron(nc, *args)
    r = _run(nc, [arrays], core_ids=[0])
    return r.results[0]["out_0_dram"]
```

```python
import numpy as np
import concourse.bass as bass
from concourse import mybir
from contextlib import ExitStack

TOKENS, DIM, HEADS, HEAD_DIM = 8192, 128, 16, 64
SEQ, WINDOW = 256, 32
GROUP = 512
GROUPS = TOKENS // GROUP
TILES = GROUP // 128
BLOCKS = GROUP // WINDOW
QUADS = BLOCKS // 4
LOOPS = (GROUPS - 6) // 2
HQ = HEADS * WINDOW
EPS = 1e-5
NEG = -1e30
T_HEADS = [range(0, 6), range(6, 11), range(11, 16), range(0)]
C_IDENT, C_EYE, C_MASK, C_BLOCK, C_LOW, C_END = 0, 128, 160, 416, 544, 545


def constants():
    p = np.arange(128)
    c = np.zeros((128, C_END), np.float32)
    c[:, C_IDENT:C_IDENT + 128] = np.eye(128)
    c[:, C_EYE:C_EYE + 32] = (p[:, None] % 32) == np.arange(32)[None]
    query, key = p[:, None] % 32, p[None] % 64
    seen = (key >= query) & (key <= query + WINDOW)
    c[:, C_MASK:C_MASK + 128] = np.where(seen, 0.0, NEG)
    c[:, C_MASK + 128:C_MASK + 256] = np.where(seen & ((p[None] >= 64) | (key >= 32)), 0.0, NEG)
    c[:, C_BLOCK:C_BLOCK + 128] = (p[:, None] // 64) == (p[None] // 64)
    c[:, C_LOW] = (p // 32) % 2
    return c


def macaron(nc, x_in, gamma, w_qkv, w_gates, b_gates, w_out, w_r, w_k, w_v, mu_r, mu_k, consts, out):
    dt = mybir.dt
    f32, f32r, bf16, f16, i32 = dt.float32, dt.float32r, dt.bfloat16, dt.float16, dt.int32
    ALU, ACT, AX = mybir.AluOpType, mybir.ActivationFunctionType, mybir.AxisListType

    x_tiles = x_in.rearrange("b (n p) c -> p (b n) c", p=128)
    out_tiles = out.rearrange("b (n p) c -> p (b n) c", p=128)

    ctx = ExitStack()
    with ctx:
        def sb(name, shape, dtype=f32):
            return ctx.enter_context(nc.sbuf_tensor(name, shape, dtype))

        def sem(name):
            return ctx.enter_context(nc.semaphore(name))

        cst = sb("cst", [128, C_END])
        ident = cst[:, C_IDENT:C_IDENT + 128]
        eye = cst[:, C_EYE:C_EYE + 32]
        eye_bf = sb("eye_bf", [128, 32], bf16)
        mask_bf = sb("mask_bf", [128, 2, 128], bf16)
        minus_bf = sb("minus_bf", [128, 128], bf16)
        ones_r = sb("ones_r", [128, 128], f32r)
        minus_low = sb("minus_low", [128, 1])
        gam = sb("gam", [128, 1])
        mu = sb("mu", [128, 2])
        gate_bias = sb("gate_bias", [128, HEADS])
        wg = sb("wg", [128, HEADS])
        fold_qk = [sb(n, [128, HEADS, 128], f32r) for n in ("fold_qk_hi", "fold_qk_lo")]
        fold_vo = sb("fold_vo", [128, HEADS, 128])
        ffn_wT = sb("ffn_wT", [128, 3, 128])
        x = sb("x", [128, TOKENS // 128, DIM])
        t = [sb(f"t{i}", [128, HEADS, GROUP]) for i in range(2)]
        zT = [sb(f"zT{i}", [128, WINDOW + GROUP]) for i in range(2)]
        zk = [sb(f"zk{i}", [128, BLOCKS, 2, DIM], f16) for i in range(2)]
        zT_hi = sb("zT_hi", [128, GROUP], f32r)
        zT_lo = sb("zT_lo", [128, GROUP], f32r)
        z_parts = sb("z_parts", [128, TILES, 2, DIM], f16)
        gate_rows = sb("gate_rows", [128, TILES, HEADS])
        U = sb("U", [128, HEADS, 4, WINDOW])
        z = sb("z", [128, TILES, DIM])
        P = [sb(f"P{i}", [128, 2 * HQ]) for i in range(2)]
        P_even = sb("P_even", [128, 2, HQ], f16)
        P_odd = sb("P_odd", [128, 2, HQ], f16)
        shift_rows = sb("shift_rows", [128, 2, HQ], bf16)
        factor_rows = sb("factor_rows", [128, 2, HQ], f32r)
        half = sb("half", [128, 32])
        swapped = sb("swapped", [128, 32])
        m_full = sb("m_full", [128, 32])
        m_hi = sb("m_hi", [128, 32], bf16)
        m_parts = sb("m_parts", [128, 32], bf16)
        den = sb("den", [128, 32])
        f_full = sb("f_full", [128, 32])
        f_hi = sb("f_hi", [128, 32], f32r)
        f_parts = sb("f_parts", [128, 32])
        gate = [sb(f"gate{i}", [128, 8, HEADS]) for i in range(2)]
        stats = sb("stats", [128, TILES, 6])
        mean_var = sb("mean_var", [128, TILES, 2])
        ra, rt = (sb(n, [128, TILES]) for n in ("ra", "rt"))
        nscale, nbias = (sb(n, [128, 3, TILES]) for n in ("nscale", "nbias"))
        pause = sb("pause", [128, 1])
        act_pause = sb("act_pause", [128, 3])
        pool_pause = sb("pool_pause", [128, 1])
        y = [sb(f"y{i}", [128, TILES, DIM]) for i in range(2)]
        yT = [sb(f"yT{i}", [128, 2, SEQ + 1]) for i in range(2)]
        xr = [sb(f"xr{i}", [128, GROUP]) for i in range(2)]
        xk = [sb(f"xk{i}", [128, GROUP]) for i in range(2)]
        kact = [sb(f"kact{i}", [128, GROUP]) for i in range(2)]
        tanh_r = [sb(f"tanh_r{i}", [128, GROUP]) for i in range(2)]
        stage = t[1][:, :, :].rearrange("p h n -> p (h n)")
        wqkv_st = stage[:, 0:3072]
        wT_st = stage[:, 3072:6144].rearrange("p (j c) -> p j c", c=128)
        wout_st = stage[:, 6144:7168].rearrange("p (j c) -> p j c", c=128)
        ffn_st = stage[:, 7168:7552].rearrange("p (j c) -> p j c", c=128)

        ps = ctx.enter_context(nc.psum_tensor("ps", [128, 8, 512], f32))
        S = [ps[:, 0:2, :], ps[:, 2:4, :]]
        prod = [ps[:, 4 + i, :] for i in range(3)]
        wbank = ps[:, 7, :]
        obank = wbank[:, 0:128]

        s_const, s_ffn_weights, s_weights, s_load0, s_load1, s_loadrest = (sem(n) for n in ("s_const", "s_ffn_weights", "s_weights", "s_load0", "s_load1", "s_loadrest"))
        s_scaled, s_tr, s_trc, s_fold, s_set = (sem(n) for n in ("s_scaled", "s_tr", "s_trc", "s_fold", "s_set"))
        s_pad = sem("s_pad")
        s_scores, s_m, s_shiftrows, s_shift, s_exp = (sem(n) for n in ("s_scores", "s_m", "s_shiftrows", "s_shift", "s_exp"))
        s_f, s_factorrows, s_factor, s_scaled_p = (sem(n) for n in ("s_f", "s_factorrows", "s_factor", "s_scaled_p"))
        s_phi_odd, s_phi_even, s_plo_even, s_plo_odd = (sem(n) for n in ("s_phi_odd", "s_phi_even", "s_plo_even", "s_plo_odd"))
        s_prod, s_evac, s_out, s_outadd = (sem(n) for n in ("s_prod", "s_evac", "s_out", "s_outadd"))
        s_z, s_zTp, s_zT, s_zTlo, s_zhi, s_zlo, s_zk = (
            sem(n) for n in ("s_z", "s_zTp", "s_zT", "s_zTlo", "s_zhi", "s_zlo", "s_zk"))
        s_gp, s_g, s_gexp, s_gate = (sem(n) for n in ("s_gp", "s_g", "s_gexp", "s_gate"))
        s_zstat = sem("s_zstat")
        s_stat, s_diff, s_y, s_yTp, s_yT, s_mix, s_kp, s_relu, s_kact, s_rp, s_th, s_vp, s_gv, s_x = (
            [sem(f"{n}{i + 1}") for i in range(2)]
            for n in ("s_stat", "s_diff", "s_y", "s_yTp", "s_yT", "s_mix", "s_kp", "s_relu", "s_kact", "s_rp", "s_th", "s_vp", "s_gv", "s_x"))
        s_link, s_store = sem("s_link"), sem("s_store")

        def attends(s):
            return 0 <= s < GROUPS

        def exists(s, q):
            return 0 <= QUADS * s + q + 1 < QUADS * GROUPS

        def products_before(g, s):
            if s < 0:
                return 0
            return HEADS * (s < GROUPS) + (HEADS + BLOCKS) * g

        def has_before(s, q):
            return 0 <= QUADS * s + q - 1 < QUADS * GROUPS

        def loop_slots(engine, slot):
            for s in (-2, -1, 0, 1):
                slot(s, s)
            with engine.Fori(0, LOOPS) as it:
                for k in range(2):
                    slot(it * 2 + (2 + k), 2 + k)
            for s in range(2 + 2 * LOOPS, GROUPS + 1):
                slot(s, s)

        def fold_heads(dst, odd, hb):
            return dst[:, 8 * hb + odd:8 * hb + odd + 7:2, :]

        def fold_bank(k, odd, hb):
            return ps[:, 4 * k + 2 * odd + hb, :].rearrange("p (j c) -> p j c", c=128)

        block = ctx.enter_context(nc.Block())

        @block.sync
        def _(sp):
            sp.dma_start(x[:, 0:TILES, :], x_tiles[:, 0:TILES, :]).then_inc(s_load0, 16)
            sp.dma_start(ffn_st[:, 0, :], w_r).then_inc(s_ffn_weights, 16)
            sp.dma_start(ffn_st[:, 1, :], w_k).then_inc(s_ffn_weights, 16)
            sp.dma_start(ffn_st[:, 2, :], w_v).then_inc(s_ffn_weights, 16)
            sp.dma_start(cst[:, :], consts).then_inc(s_const, 16)
            sp.dma_start(wqkv_st, w_qkv).then_inc(s_weights, 16)
            sp.dma_start(x[:, TILES:2 * TILES, :], x_tiles[:, TILES:2 * TILES, :]).then_inc(s_load1, 16)
            sp.dma_start(wout_st, w_out.rearrange("(j p) c -> p j c", p=128)).then_inc(s_weights, 16)
            sp.dma_start(x[:, 2 * TILES:, :], x_tiles[:, 2 * TILES:, :]).then_inc(s_loadrest, 16)

            def slot(g, s):
                cur = s % 2
                if attends(s + 2):
                    sp.wait_ge(s_zhi, g + 3)
                    sp.wait_ge(s_zlo, g + 3)
                    if s >= 0:
                        sp.wait_ge(s_evac, products_before(g + 1, s + 1))
                    for j in range(4):
                        src = z_parts[32 * j:32 * j + 32, :, :, :]
                        for a in range(2):
                            sp.dma_start(zk[cur][64 * a + 32:64 * a + 64, j:BLOCKS:4, :, :], src).then_inc(s_zk, 16)
                            n = TILES if j < 3 else TILES - 1
                            sp.dma_start(zk[cur][64 * a:64 * a + 32, j + 1:BLOCKS:4, :, :], src[:, 0:n]).then_inc(s_zk, 16)
                    sp.wait_ge(s_gexp, g + 3)
                    for j in range(4):
                        for a in range(2):
                            d = 64 * (j % 2) + 32 * a
                            sp.dma_start(gate[cur][d:d + 32, j // 2:8:2, :], gate_rows[32 * j:32 * j + 32, :, :]
                                         ).then_inc(s_gate, 16)
                if attends(s - 1):
                    sp.wait_ge(s_x[1], g)
                    rows = bass.ds(TILES * (g - 1), TILES)
                    sp.dma_start(out_tiles[:, rows, :], x[:, rows, :]).then_inc(s_store, 16)

            loop_slots(sp, slot)
            sp.wait_ge(s_store, 16 * GROUPS)

        @block.tensor
        def _(pe):
            mm = pe.matmul
            pe.wait_ge(s_const, 16)
            pe.wait_ge(s_ffn_weights, 16 * 5)
            for j in range(3):
                i = pe.transpose(wbank[:, 128 * j:128 * j + 128], ffn_st[:, j, :], ident)
            i.then_inc(s_tr, 1)

            def transpose_weights():
                pe.wait_ge(s_scaled, 1)
                for b in range(6):
                    for j in range(4):
                        c = 128 * (4 * b + j)
                        i = pe.transpose(ps[:, b, 128 * j:128 * j + 128], wqkv_st[:, c:c + 128], ident)
                    i.then_inc(s_tr, 1)

            def fold_weights():
                pe.wait_ge(s_trc, 7)
                pe.wait_ge(s_gv[0], 1)
                for k, (a, b) in enumerate(((lambda j: wT_st[:, j, :], lambda j: wT_st[:, 8 + j, :]),
                                            (lambda j: wT_st[:, 16 + j, :], lambda j: wout_st[:, j, :]))):
                    for h in range(HEADS):
                        j, r = h // 2, (h % 2) * 64
                        bank, col = 4 * k + 2 * (h % 2) + j // 4, 128 * (j % 4)
                        i = mm(ps[:, bank, col:col + 128], a(j)[r:r + 64, :], b(j)[r:r + 64, :], start=True, stop=True)
                    i.then_inc(s_fold, 1)
                pe.wait_ge(s_set, 3)
                release[0] = None

            release = [(s_trc, 1)]

            def take_work_bank():
                if release[0] is not None:
                    pe.wait_ge(*release[0])

            def work_transposes(src, done, value, freed, made, made_value):
                pe.wait_ge(made, made_value)
                take_work_bank()
                for i in range(TILES):
                    op = pe.transpose(wbank[:, 128 * i:128 * i + 128], src[:, i, :], ident)
                op.then_inc(done, 1)
                release[0] = (freed, value)

            def slot(g, s):
                has_next, has_ffn1, has_ffn2 = attends(s + 1), attends(s + 2), attends(s - 1)
                cur, nxt = s % 2, (s + 1) % 2
                if s > -2:
                    release[0] = (s_gv[1], g - 1) if s >= 2 else (s_zT, g + 2)
                count = [0, 0]

                def product():
                    if count[1] >= 3:
                        pe.wait_ge(s_evac, products_before(g, s) + count[0] - 2)
                    bank = prod[count[1] % 3]
                    count[0] += 1
                    count[1] += 1
                    return bank

                def gates():
                    if not has_next or s == -2:
                        return
                    pe.wait_ge(s_zT, g + 2)
                    take_work_bank()
                    for i in range(TILES):
                        tokens = zT[nxt][:, WINDOW + 128 * i:WINDOW + 128 * i + 128]
                        op = mm(wbank[:, 16 * i:16 * i + 16], tokens, wg[:, :], start=True, stop=True)
                        if i < TILES - 1:
                            yield
                    op.then_inc(s_gp, 1)
                    release[0] = (s_g, g + 2)
                    yield

                def ffn(layer, gg, stage_):
                    if not (has_ffn1 if layer == 0 else has_ffn2):
                        return
                    if stage_[0] == "T":
                        return work_transposes(y[layer], s_yTp[layer], gg + 1, s_yT[layer], s_y[layer], gg + 1)
                    if stage_ == "k":
                        pe.wait_ge(s_mix[layer], gg + 1)
                        take_work_bank()
                        mm(wbank, ffn_wT[:, 1, :], xk[layer][:, :], start=True, stop=True).then_inc(s_kp[layer], 1)
                        release[0] = (s_relu[layer], gg + 1)
                    if stage_ == "r":
                        take_work_bank()
                        for i in range(TILES):
                            c = slice(128 * i, 128 * i + 128)
                            op = mm(wbank[:, c], xr[layer][:, c], ffn_wT[:, 0, :], start=True, stop=True)
                        op.then_inc(s_rp[layer], 1)
                        release[0] = (s_th[layer], gg + 1)
                    if stage_ == "v":
                        pe.wait_ge(s_kact[layer], gg + 1)
                        take_work_bank()
                        for i in range(TILES):
                            c = slice(128 * i, 128 * i + 128)
                            op = mm(wbank[:, c], kact[layer][:, c], ffn_wT[:, 2, :], start=True, stop=True)
                        op.then_inc(s_vp[layer], 1)
                        release[0] = (s_gv[layer], gg + 1)

                def z_transposes():
                    if has_ffn1:
                        work_transposes(z, s_zTp, g + 3, s_zT, s_z, g + 3)

                work = [{"early": lambda: ffn(0, g + 2, "T"), "last": lambda: ffn(0, g + 2, "k")},
                        {"late": lambda: ffn(0, g + 2, "r"), "within": lambda: ffn(0, g + 2, "v"),
                         "last": lambda: ffn(1, g - 1, "T")},
                        {"within": lambda: ffn(1, g - 1, "k"), "last": lambda: ffn(1, g - 1, "r")},
                        {"late": z_transposes, "within": lambda: ffn(1, g - 1, "v")}]

                def do(q, when):
                    if when in work[q]:
                        work[q][when]()

                def scores(q):
                    nq, par = (q + 1) % 4, (q + 1) % 2
                    own = cur if q < 3 else nxt
                    for i in range(2):
                        first = nq % 2 == 0 and i == 0
                        rows = slice(32 * i, 32 * i + 32)
                        every_head = eye_bf[rows, :].unsqueeze(1).to_broadcast([32, HEADS, 32])
                        mm(S[par][:, i, :], mask_bf[rows, int(first), :], every_head, start=True, stop=False,
                           skip_group_check=True)
                    if q == 3:
                        pe.wait_ge(s_evac, products_before(g, s) + count[0] - 4 * attends(s))
                    for i in range(2):
                        for j in range(2):
                            b = 4 * nq + 2 * i + j
                            op = mm(S[par][64 * j:64 * j + 64, i, :], zT[own][:, 32 * b:32 * b + 64],
                                    t[own][:, :, 32 * b:32 * b + 32], start=False, stop=True, skip_group_check=True)
                        op.then_inc(s_scores, 1)
                        if q == 0:
                            next(gate_products, None)
                            next(gate_products, None)

                def factors(q):
                    for i in range(2):
                        pe.wait_ge(s_factorrows, 2 * (QUADS * g + q) + 1 + i)
                        op = mm(S[q % 2][:, i, :], ones_r[:, :], factor_rows[:, i, :], start=True, stop=True)
                    op.then_inc(s_factor, 1)

                gate_products = gates()
                for q in range(QUADS):
                    quad = QUADS * g + q
                    new = exists(s, q)
                    par = (q + 1) % 2
                    if new and not (s == GROUPS - 1 and q > 0):
                        scores(q)
                    if q == 0:
                        for _ in gate_products:
                            pass
                    if attends(s):
                        factors(q)
                    count[1] = 0
                    if s >= 0 or count[0]:
                        pe.wait_ge(s_evac, products_before(g, s) + count[0])
                    if has_before(s, q):
                        take_work_bank()
                        for h in range(HEADS):
                            op = mm(obank, U[:, h, :, :].rearrange("p b q -> p (b q)"), fold_vo[:, h, :],
                                    start=(h == 0), stop=(h == HEADS - 1))
                        op.then_inc(s_out, 1)
                        release[0] = (s_outadd, quad)

                    heads = list(T_HEADS[q]) if has_next else []

                    def folded_query():
                        h = heads.pop(0)
                        bank = product()
                        mm(bank, fold_qk[1][:, h, :], zT_hi[:, :], start=True, stop=False)
                        mm(bank, fold_qk[0][:, h, :], zT_lo[:, :], start=False, stop=False)
                        mm(bank, fold_qk[0][:, h, :], zT_hi[:, :], start=False, stop=True).then_inc(s_prod, 1)

                    if has_next and q == 0:
                        pe.wait_ge(s_zTlo, g + 2)
                    if new:
                        for i in range(2):
                            pe.wait_ge(s_shiftrows, 2 * quad + 3 + i)
                            op = mm(S[par][:, i, :], minus_bf[:, :], shift_rows[:, i, :], start=False, stop=True,
                                    skip_group_check=True)
                            op.then_inc(s_shift, 1)
                            if i == 0 and heads:
                                folded_query()
                    do(q, "early")
                    while heads:
                        folded_query()
                    do(q, "late")
                    if s == GROUPS - 1 and exists(s, q + 1) and q < 3:
                        pe.wait_ge(s_scaled_p, quad + 1)
                        scores(q + 1)
                    if attends(s):
                        if q == 0:
                            pe.wait_ge(s_zk, 256 * (g + 1))
                        for pair in range(2):
                            b = 4 * q + 2 * pair
                            even = product()
                            pe.wait_ge(s_phi_even, quad + 1)
                            mm(even, zk[cur][0:64, b, 1, :], P_even[0:64, pair, :], start=True, stop=False)
                            odd = product()
                            pe.wait_ge(s_phi_odd, quad + 1)
                            mm(odd, zk[cur][64:128, b + 1, 1, :], P_odd[64:128, pair, :], start=True, stop=False)
                            pe.wait_ge(s_plo_even, 2 * quad + 1 + pair)
                            mm(even, zk[cur][:, b, 0, :], P_even[:, pair, :], start=False, stop=True).then_inc(s_prod, 1)
                            pe.wait_ge(s_plo_odd, 2 * quad + 1 + pair)
                            mm(odd, zk[cur][:, b + 1, 0, :], P_odd[:, pair, :], start=False, stop=True).then_inc(s_prod, 1)
                            if pair == 0:
                                do(q, "within")
                    else:
                        do(q, "within")
                    do(q, "last")
                    if (s, q) == (-2, 0):
                        transpose_weights()
                    if (s, q) == (-2, 1):
                        fold_weights()

            loop_slots(pe, slot)

        @block.scalar
        def _(act):
            def wait(sem_, value):
                act.wait_ge(sem_, value)
                act.wait_ge(s_const, 16)

            act.dma_start(mu[:, 0:1], mu_r.rearrange("(p a) -> p a", a=1)).then_inc(s_ffn_weights, 16)
            act.dma_start(mu[:, 1:2], mu_k.rearrange("(p a) -> p a", a=1)).then_inc(s_ffn_weights, 16)
            act.dma_start(gam[:, :], gamma.rearrange("(p a) -> p a", a=1)).then_inc(s_weights, 16)
            act.dma_start(wg[:, :], w_gates).then_inc(s_weights, 16)
            act.dma_start(gate_bias[:, :], b_gates.rearrange("(a h) -> a h", a=1).to_broadcast([128, HEADS])
                          ).then_inc(s_weights, 16)
            act.wait_ge(s_tr, 1)
            act.activation(ffn_wT[:, 0:2, :], wbank[:, 0:256].rearrange("p (j c) -> p j c", c=128), ACT.Copy)
            act.activation(ffn_wT[:, 2, :], wbank[:, 256:384], ACT.Copy, scale=0.25).then_inc(s_trc, 1)

            def copy_transposes():
                for b in range(6):
                    act.wait_ge(s_tr, b + 2)
                    act.activation(wT_st[:, 4 * b:4 * b + 4, :], ps[:, b, :].rearrange("p (j c) -> p j c", c=128),
                                   ACT.Copy, scale=HEAD_DIM ** -0.5 if b < 2 else 1.0).then_inc(s_trc, 1)

            def copy_folded():
                for k, dst in enumerate((fold_qk[0], fold_vo)):
                    act.wait_ge(s_fold, k + 1)
                    for odd in range(2):
                        for hb in range(2):
                            op = act.activation(fold_heads(dst, odd, hb), fold_bank(k, odd, hb), ACT.Copy)
                    op.then_inc(s_set, 1)

            act.wait_ge(s_pad, 1)

            def normalise(which, dst, gg, ready, done):
                wait(ready, gg + 1)
                act.activation(act_pause[:, which:which + 1], cst[:, 0:1], ACT.Copy)
                for i in range(TILES):
                    rows = x[:, bass.ds(TILES * gg + i, 1), :]
                    op = act.activation(dst[:, i:i + 1, :], rows, ACT.Identity, scale=nscale[:, which, i:i + 1],
                                        bias=nbias[:, which, i:i + 1])
                op.then_inc(done, 1)

            def slot(g, s):
                has_next, has_ffn1, has_ffn2 = attends(s + 1), attends(s + 2), attends(s - 1)
                cur, nxt = s % 2, (s + 1) % 2
                count = [0, 0]

                def evacuate(dst, by_head=False):
                    n = products_before(g, s) + count[0]
                    wait(s_prod, n + 1)
                    src = prod[count[1] % 3]
                    if by_head:
                        src = src.rearrange("p (h q) -> p h q", q=WINDOW)
                    act.activation(dst, src, ACT.Copy).then_inc(s_evac, 1)
                    count[0] += 1
                    count[1] += 1

                def ffn(layer, gg, stage_):
                    if not (has_ffn1 if layer == 0 else has_ffn2):
                        return
                    if stage_[0] == "T":
                        wait(s_yTp[layer], gg + 1)
                        act.activation(yT[layer][:, :, 1:], wbank.rearrange("p (b n) -> p b n", b=2),
                                       ACT.Copy).then_inc(s_yT[layer], 1)
                    if stage_ == "k":
                        wait(s_kp[layer], gg + 1)
                        act.activation(kact[layer][:, :], wbank, ACT.Relu).then_inc(s_relu[layer], 1)
                    if stage_ == "r":
                        if s + (2 if layer == 0 else -1) > 0:
                            wait(s_x[layer], gg)
                        wait(s_rp[layer], gg + 1)
                        act.activation(tanh_r[layer][:, :], wbank, ACT.Tanh, scale=0.5).then_inc(s_th[layer], 1)

                def z_out():
                    if has_ffn1:
                        wait(s_zTp, g + 3)
                        act.activation(zT[cur][:, WINDOW:], wbank, ACT.Copy).then_inc(s_zT, 1)
                        if s > -2:
                            wait(s_zk, 256 * (g + 2))
                        act.activation(z_parts[:, :, 0, :], z[:, :, :], ACT.Copy).then_inc(s_zhi, 1)

                def gates():
                    if has_ffn1:
                        wait(s_g, g + 3)
                        act.activation(gate_rows[:, :, :], gate_rows[:, :, :], ACT.Exp, scale=-1.0).then_inc(s_gexp, 1)

                for q in range(QUADS):
                    quad = QUADS * g + q
                    count[1] = 0
                    if q == 1 and has_ffn2:
                        normalise(1, y[1], g - 1, s_stat[1], s_y[1])
                    if attends(s):
                        wait(s_scaled_p, quad + 1)
                        pairs = P[q % 2][:, :].rearrange("p (a n) -> p a n", a=2)
                        act.activation(P_odd[64:128], pairs[64:128], ACT.Copy).then_inc(s_phi_odd, 1)
                    heads = list(T_HEADS[q]) if has_next else []
                    if heads and q == 0 and s > 0:
                        wait(s_scores, 8 * g)
                    if exists(s, q):
                        for i in range(2):
                            wait(s_shift, 2 * quad + 3 + i)
                            act.activation(P[(q + 1) % 2][:, HQ * i:HQ * i + HQ], S[(q + 1) % 2][:, i, :],
                                           ACT.Exp).then_inc(s_exp, 1)
                            if i == 0 and heads:
                                evacuate(t[nxt][:, heads.pop(0), :])
                    if q == 0:
                        ffn(0, g + 2, "T")
                    for h in heads:
                        evacuate(t[nxt][:, h, :])
                    if q == 1:
                        ffn(0, g + 2, "r")
                    if q == 3:
                        z_out()
                    for pair in range(2):
                        if attends(s):
                            evacuate(U[:, :, 2 * pair, :], True)
                            evacuate(U[:, :, 2 * pair + 1, :], True)
                        if q == 2 and pair == 0:
                            ffn(1, g - 1, "k")
                    if q == 0:
                        ffn(0, g + 2, "k")
                        if s == -2:
                            copy_transposes()
                    if q == 1:
                        ffn(1, g - 1, "T")
                        if s == -2:
                            copy_folded()
                    if q == 2:
                        ffn(1, g - 1, "r")
                        if attends(s + 3):
                            normalise(0, y[0], g + 3, s_stat[0], s_y[0])
                        if has_ffn1:
                            normalise(2, z, g + 2, s_zstat, s_z)
                    if q == 3:
                        gates()

            normalise(0, y[0], 0, s_stat[0], s_y[0])
            loop_slots(act, slot)

        @block.vector
        def _(dve):
            links = [0, 0]

            def link(op):
                links[0] += 1
                count = links[0] + links[1]
                op.then_inc(s_link, 1)
                yield
                dve.wait_ge(s_link, count)

            def together(*chains):
                chains = list(chains)
                while chains:
                    chains = [c for c in chains if next(c, "end") != "end"]

            dve.memset(zT[0][:, 0:WINDOW], 0.0)
            dve.memset(zT[1][:, 0:WINDOW], 0.0)
            for i in range(2):
                dve.memset(zk[i][:, 0:1, :, :], 0.0)
            for i in range(2):
                op = dve.memset(yT[i][:, :, 0:1], 0.0)
            op.then_inc(s_pad, 1)

            def scale_weights():
                dve.wait_ge(s_weights, 16 * 5)
                together(link(dve.tensor_scalar(wg[:, :], wg[:, :], gam[:, 0:1], None, ALU.mult)))
                dve.tensor_scalar(wqkv_st, wqkv_st, gam[:, 0:1], None, ALU.mult).then_inc(s_scaled, 1)

            def fold_low():
                dve.wait_ge(s_set, 1)
                for odd in range(2):
                    for hb in range(2):
                        op = dve.tensor_tensor(fold_heads(fold_qk[1], odd, hb), fold_bank(0, odd, hb),
                                               fold_heads(fold_qk[0], odd, hb).bitcast(f32), ALU.subtract)
                op.then_inc(s_set, 1)

            def copy_constants():
                dve.wait_ge(s_const, 16)
                dve.tensor_copy(eye_bf[:, :], eye)
                dve.tensor_copy(mask_bf[:, :, :], cst[:, C_MASK:C_MASK + 256].rearrange("p (k n) -> p k n", k=2))
                dve.tensor_scalar(minus_bf[:, :], cst[:, C_BLOCK:C_BLOCK + 128], -1.0, None, ALU.mult)
                dve.tensor_copy(ones_r[:, :], cst[:, C_BLOCK:C_BLOCK + 128])
                dve.tensor_scalar(minus_low[:, :], cst[:, C_LOW:C_LOW + 1], -1.0, None, ALU.mult)

            def statistics(first_tile, which, done):
                dve.memset(pause[:, :], 0.0)
                for i in range(TILES):
                    op = dve.bn_stats(stats[:, i, :], x[:, bass.ds(first_tile + i, 1), :])
                yield from link(op)
                dve.memset(pause[:, :], 0.0)
                for i in range(TILES):
                    op = dve.bn_aggr(mean_var[:, i, :], stats[:, i, :])
                yield from link(op)
                var, root, bias = mean_var[:, :, 1], nscale[:, which, :], nbias[:, which, :]
                if which == 2:
                    yield from link(dve.tensor_scalar(ra[:, :], var, EPS, 1e-24 / DIM, ALU.add, ALU.mult))
                    yield from link(dve.tensor_tensor(ra[:, :], var, ra[:, :], ALU.max))
                else:
                    yield from link(dve.tensor_scalar(ra[:, :], var, EPS, None, ALU.add))
                yield from link(dve.tensor_scalar(root.bitcast(i32), ra[:, :].bitcast(i32), -0.5, float(0x5F3759DF),
                                       ALU.mult, ALU.add))
                for _ in range(3):
                    yield from link(dve.tensor_tensor(rt[:, :], root, root, ALU.mult))
                    yield from link(dve.scalar_tensor_tensor(rt[:, :], rt[:, :], -0.5, ra[:, :], ALU.mult, ALU.mult))
                    yield from link(dve.scalar_tensor_tensor(root, rt[:, :], 1.5, root, ALU.add, ALU.mult))
                dve.scalar_tensor_tensor(bias, mean_var[:, :, 0], -1.0, root, ALU.mult, ALU.mult).then_inc(done, 1)

            def swap_halves():
                for i in range(4):
                    a, b = 32 * i, 32 * (i ^ 1)
                    op = dve.tensor_copy(swapped[a:a + 32, :], half[b:b + 32, :])
                yield from link(op)

            def slot(g, s):
                has_next, has_ffn1, has_ffn2 = attends(s + 1), attends(s + 2), attends(s - 1)
                cur, nxt = s % 2, (s + 1) % 2

                def prepare_first(s_, gg):
                    if attends(s_):
                        if s_ < 3:
                            dve.wait_ge((s_load0, s_load1, s_loadrest)[s_], 16)
                        yield from statistics(TILES * gg, 0, s_stat[0])

                def prepare_second():
                    if has_ffn2:
                        dve.wait_ge(s_outadd, 4 * g)
                        yield from statistics(TILES * (g - 1), 1, s_stat[1])

                def mix(layer, gg):
                    if not (has_ffn1 if layer == 0 else has_ffn2):
                        return
                    dve.wait_ge(s_diff[layer], gg + 1)
                    before = yT[layer][:, :, 0:SEQ]
                    diff = xk[layer][:, :].rearrange("p (b n) -> p b n", b=2)
                    dve.scalar_tensor_tensor(xr[layer][:, :].rearrange("p (b n) -> p b n", b=2), diff,
                                             mu[:, 0:1], before, ALU.mult, ALU.add)
                    dve.scalar_tensor_tensor(diff, diff, mu[:, 1:2], before, ALU.mult, ALU.add).then_inc(s_mix[layer], 1)

                def gated(layer, gg):
                    if not (has_ffn1 if layer == 0 else has_ffn2):
                        return
                    dve.wait_ge(s_th[layer], gg + 1)
                    dve.wait_ge(s_vp[layer], gg + 1)
                    dve.scalar_tensor_tensor(tanh_r[layer][:, :], tanh_r[layer][:, :], 1.0, wbank, ALU.add,
                                             ALU.mult).then_inc(s_gv[layer], 1)

                def prepare_z():
                    if has_ffn1:
                        dve.wait_ge(s_x[0], g + 3)
                        yield from statistics(TILES * (g + 2), 2, s_zstat)

                def z_low():
                    if has_ffn1:
                        dve.wait_ge(s_zT, g + 3)
                        yield from link(dve.tensor_copy(zT_hi[:, :], zT[cur][:, WINDOW:]))
                        dve.tensor_tensor(zT_lo[:, :], zT[cur][:, WINDOW:], zT_hi[:, :].bitcast(f32), ALU.subtract
                                          ).then_inc(s_zTlo, 1)

                def z_parts_low():
                    if has_ffn1:
                        dve.wait_ge(s_zhi, g + 3)
                        dve.tensor_tensor(z_parts[:, :, 1, :], z[:, :, :], z_parts[:, :, 0, :], ALU.subtract
                                          ).then_inc(s_zlo, 1)
                        yield

                def gates():
                    if has_ffn1:
                        dve.wait_ge(s_gp, g + 3)
                        if s > -2:
                            dve.wait_ge(s_gate, 128 * (g + 2))
                        dve.tensor_tensor(gate_rows[:, :, :], wbank[:, 0:64].rearrange("p (a h) -> p a h", h=HEADS),
                                          gate_bias[:, :].unsqueeze(1).to_broadcast([128, TILES, HEADS]),
                                          ALU.add).then_inc(s_g, 1)

                def add_output(first_tile, quad):
                    dve.wait_ge(s_out, quad + 1)
                    dve.tensor_tensor(x[:, bass.ds(first_tile, 1), :], x[:, bass.ds(first_tile, 1), :],
                                      obank.unsqueeze(1), ALU.add).then_inc(s_outadd, 1)

                before_den = [[], [], [lambda: mix(1, g - 1)], []]
                beside_den = [prepare_second, lambda: prepare_first(s + 3, g + 3), prepare_z, lambda: iter(())]
                after_den = [[lambda: mix(0, g + 2)],
                             [lambda: gated(0, g + 2)],
                             [],
                             [lambda: gated(1, g - 1), lambda: together(z_low(), z_parts_low()), gates]]

                def maxima(q):
                    for i in range(2):
                        dve.wait_ge(s_scores, 2 * (QUADS * g + q + 2) - 1 + i)
                        op = dve.tensor_reduce(half[:, HEADS * i:HEADS * i + HEADS],
                                               S[(q + 1) % 2][:, i, :].rearrange("p (h n) -> p h n", n=32),
                                               AX.X, ALU.max, apply_transpose=True)
                    yield from link(op)
                    yield from swap_halves()
                    dve.tensor_tensor(m_hi[:, :], half[:, :], swapped[:, :], ALU.max)
                    yield from link(dve.tensor_tensor(m_full[:, :], half[:, :], swapped[:, :], ALU.max))
                    dve.scalar_tensor_tensor(m_parts[:, :], m_hi[:, :], minus_low[:, 0:1], m_full[:, :],
                                             ALU.mult, ALU.add).then_inc(s_m, 1)

                def sums(q):
                    own, nq = (cur if q < 3 else nxt), (q + 1) % 4
                    dve.wait_ge(s_exp, 2 * (QUADS * g + q + 2))
                    if q == 3:
                        dve.wait_ge(s_gate, 128 * (g + 2))
                    yield from link(dve.tensor_reduce(half[:, :], P[(q + 1) % 2][:, :].rearrange("p (a n) -> p a n", n=32),
                                                      AX.X, ALU.add, apply_transpose=True))
                    yield from swap_halves()
                    yield from link(dve.tensor_tensor(den[:, :], half[:, :], swapped[:, :], ALU.add))
                    gates_ = gate[own][:, 2 * nq:2 * nq + 2, :].rearrange("p a h -> p (a h)")
                    yield from link(dve.scalar_tensor_tensor(den[:, :], gates_, 1.0, den[:, :], ALU.add, ALU.mult))
                    yield from link(dve.reciprocal(f_full[:, :], den[:, :]))
                    yield from link(dve.tensor_copy(f_hi[:, :], f_full[:, :]))
                    dve.scalar_tensor_tensor(f_parts[:, :], f_hi[:, :].bitcast(f32), minus_low[:, 0:1], f_full[:, :],
                                             ALU.mult, ALU.add).then_inc(s_f, 1)

                if s == -2:
                    together(prepare_first(0, 0))
                    copy_constants()
                    dve.wait_ge(s_ffn_weights, 16 * 5)
                for q in range(QUADS):
                    quad = QUADS * g + q
                    if exists(s, q):
                        together(maxima(q))
                    if attends(s):
                        dve.wait_ge(s_factor, quad + 1)
                        dve.tensor_tensor(P[q % 2][:, :], P[q % 2][:, :], S[q % 2].rearrange("p a n -> p (a n)"),
                                          ALU.mult).then_inc(s_scaled_p, 1)
                        dve.wait_ge(s_scaled_p, quad + 1)
                        pairs = P[q % 2][:, :].rearrange("p (a n) -> p a n", a=2)
                        dve.tensor_copy(P_even[0:64], pairs[0:64]).then_inc(s_phi_even, 1)
                    if has_before(s, q) and s < GROUPS - 1:
                        add_output(TILES * g + q - 1, quad - 1)
                    if attends(s):
                        dve.wait_ge(s_phi_even, quad + 1)
                        for i in range(2):
                            dve.tensor_tensor(P_even[64:128, i], pairs[0:64, i], P_even[0:64, i], ALU.subtract
                                              ).then_inc(s_plo_even, 1)
                    if has_before(s, q) and s >= GROUPS - 1:
                        add_output(TILES * g + q - 1, quad - 1)
                    for task in before_den[q]:
                        task()
                    beside = beside_den[q]()
                    if exists(s, q):
                        for _ in sums(q):
                            if q > 0:
                                next(beside, None)
                    elif q == 1:
                        together(beside)
                    for task in after_den[q]:
                        task()
                    together(beside)
                    if (s, q) == (-2, 0):
                        scale_weights()
                    if (s, q) == (-2, 2):
                        fold_low()

            for s in (-2, -1, 0, 1):
                slot(s, s)
            base = links[0]
            links[0] = 0
            with dve.Fori(0, LOOPS) as it:
                links[1] = it * LINKS + base
                for k in range(2):
                    slot(it * 2 + (2 + k), 2 + k)
            assert links[0] == LINKS, links[0]
            links[0], links[1] = base + LOOPS * LINKS, 0
            for s in range(2 + 2 * LOOPS, GROUPS + 1):
                slot(s, s)

        @block.gpsimd
        def _(pool):
            pool.wait_ge(s_const, 16)

            def diagonal(dst, parts, done):
                for i in range(2):
                    op = pool.tensor_tensor(dst[:, i, :].rearrange("p (h q) -> p h q", q=32),
                                            eye.unsqueeze(1).to_broadcast([128, HEADS, 32]),
                                            parts[:, 16 * i:16 * i + 16].unsqueeze(2).to_broadcast([128, HEADS, 32]),
                                            ALU.mult)
                    op.then_inc(done, 1)

            def slot(g, s):
                has_ffn1, has_ffn2 = attends(s + 2), attends(s - 1)

                def difference(layer, gg):
                    if has_ffn1 if layer == 0 else has_ffn2:
                        pool.wait_ge(s_yT[layer], gg + 1)
                        pool.tensor_tensor(xk[layer][:, :].rearrange("p (b n) -> p b n", b=2), yT[layer][:, :, 1:],
                                           yT[layer][:, :, 0:SEQ], ALU.subtract).then_inc(s_diff[layer], 1)

                def square(layer, gg):
                    if has_ffn1 if layer == 0 else has_ffn2:
                        pool.wait_ge(s_relu[layer], gg + 1)
                        pool.tensor_tensor(kact[layer][:, :], kact[layer][:, :], kact[layer][:, :],
                                           ALU.mult).then_inc(s_kact[layer], 1)

                def add(layer, gg):
                    if has_ffn1 if layer == 0 else has_ffn2:
                        pool.wait_ge(s_gv[layer], gg + 1)
                        pool.tensor_tensor(pool_pause[:, :], eye[:, 0:1], eye[:, 0:1], ALU.mult)
                        rows = x[:, bass.ds(TILES * gg, TILES), :]
                        pool.tensor_tensor(rows, rows, tanh_r[layer][:, :].rearrange("p (n c) -> p n c", c=DIM),
                                           ALU.add).then_inc(s_x[layer], 1)

                for q in range(QUADS):
                    quad = QUADS * g + q
                    if q == 1:
                        square(0, g + 2)
                    if q == 2:
                        difference(1, g - 1)
                    if q == 3:
                        square(1, g - 1)
                    if exists(s, q):
                        pool.wait_ge(s_m, quad + 2)
                        diagonal(shift_rows, m_parts, s_shiftrows)
                    if attends(s):
                        pool.drain()
                        pool.wait_ge(s_phi_odd, quad + 1)
                        pairs = P[q % 2][:, :].rearrange("p (a n) -> p a n", a=2)
                        for i in range(2):
                            pool.tensor_tensor(P_odd[0:64, i], pairs[64:128, i], P_odd[64:128, i], ALU.subtract
                                               ).then_inc(s_plo_odd, 1)
                        pool.wait_ge(s_plo_odd, 2 * quad + 2)
                    if q == 0:
                        difference(0, g + 2)
                    if exists(s, q):
                        pool.wait_ge(s_f, quad + 2)
                        diagonal(factor_rows, f_parts, s_factorrows)
                    if q == 1:
                        add(0, g + 2)
                    if q == 3:
                        add(1, g - 1)

            loop_slots(pool, slot)


LINKS = 154


_INS = ['L0_attn_x', 'L0_attn_gamma', 'L0_attn_W_qkv', 'L0_attn_W_gates', 'L0_attn_b_gates', 'L0_attn_W_out',
        'L0_ffn_W_r', 'L0_ffn_W_k', 'L0_ffn_W_v', 'L0_ffn_mu_r', 'L0_ffn_mu_k']


def kernel(**inputs):
    import numpy as _np
    import concourse.bacc as _bacc
    from concourse import mybir as _mybir
    from concourse.bass_utils import run_bass_kernel_spmd as _run

    nc = _bacc.Bacc("TRN2", target_bir_lowering=False, num_devices=1)
    arrays, args = {}, []
    named = [(n, _np.ascontiguousarray(inputs[n])) for n in _INS] + [("constants", constants())]
    for name, a in named:
        arrays[f"in_{name}_dram"] = a
        args.append(nc.dram_tensor(f"in_{name}_dram", a.shape, _mybir.dt.from_np(a.dtype), kind="ExternalInput").ap())
    args.append(nc.dram_tensor("out_0_dram", (32, 256, 128), _mybir.dt.float32, kind="ExternalOutput").ap())
    macaron(nc, *args)
    r = _run(nc, [arrays], core_ids=[0])
    return r.results[0]["out_0_dram"]
```
